# Optimizing a Trainium2 kernel written in Bass

```python
import numpy as np
import jax
import jax.numpy as jnp

def _softmax(x, axis=-1):
    return jax.nn.softmax(x, axis=axis)

def _gelu(x):
    return jax.nn.gelu(x, approximate=True)

def _silu(x):
    return jax.nn.silu(x)

def _sigmoid(x):
    return jax.nn.sigmoid(x)

def _layernorm(x, axis=-1, eps=1e-05):
    m = jnp.mean(x, axis=axis, keepdims=True)
    v = jnp.var(x, axis=axis, keepdims=True)
    return (x - m) / jnp.sqrt(v + eps)

def _scatter_add(tgt, idx, src, axis=0):
    return tgt.at[idx].add(src)

def _segment_sum(src, seg, n):
    return jax.ops.segment_sum(src, seg, n)
kernel_name = 'mk_dlrm_tower_d1_rec_r8_78af04'

def setup_inputs(seed: int=0):
    np.random.seed(seed)
    _w = jnp.asarray

    def _rec_inputs():
        import jax
        import jax.numpy as jnp
        _tk = jax.random.key(seed)
        dense_ctx = jax.random.normal(jax.random.fold_in(_tk, 190), (2048, 16), jnp.float32)
        ids = jnp.stack([jax.random.randint(jax.random.fold_in(_tk, 200 + f), (2048,), 0, v, jnp.int32) for f, v in enumerate([1000, 1000, 12500, 125000, 1250, 125000, 125000, 12500, 1000, 1250, 12500, 12500, 1250, 12500, 1000, 12500, 1250, 1250, 1000, 1000, 1250, 12500, 1000, 1000, 1250, 1250, 12500, 1000, 1000, 1250, 1000, 1000])], axis=1)
        tbl_0 = 0.05 * jax.random.normal(jax.random.fold_in(_tk, 500 + 0), (1000, 64), jnp.float32)
        tbl_1 = 0.05 * jax.random.normal(jax.random.fold_in(_tk, 500 + 1), (1000, 64), jnp.float32)
        tbl_2 = 0.05 * jax.random.normal(jax.random.fold_in(_tk, 500 + 2), (12500, 64), jnp.float32)
        tbl_3 = 0.05 * jax.random.normal(jax.random.fold_in(_tk, 500 + 3), (125000, 64), jnp.float32)
        tbl_4 = 0.05 * jax.random.normal(jax.random.fold_in(_tk, 500 + 4), (1250, 64), jnp.float32)
        tbl_5 = 0.05 * jax.random.normal(jax.random.fold_in(_tk, 500 + 5), (125000, 64), jnp.float32)
        tbl_6 = 0.05 * jax.random.normal(jax.random.fold_in(_tk, 500 + 6), (125000, 64), jnp.float32)
        tbl_7 = 0.05 * jax.random.normal(jax.random.fold_in(_tk, 500 + 7), (12500, 64), jnp.float32)
        tbl_8 = 0.05 * jax.random.normal(jax.random.fold_in(_tk, 500 + 8), (1000, 64), jnp.float32)
        tbl_9 = 0.05 * jax.random.normal(jax.random.fold_in(_tk, 500 + 9), (1250, 64), jnp.float32)
        tbl_10 = 0.05 * jax.random.normal(jax.random.fold_in(_tk, 500 + 10), (12500, 64), jnp.float32)
        tbl_11 = 0.05 * jax.random.normal(jax.random.fold_in(_tk, 500 + 11), (12500, 64), jnp.float32)
        tbl_12 = 0.05 * jax.random.normal(jax.random.fold_in(_tk, 500 + 12), (1250, 64), jnp.float32)
        tbl_13 = 0.05 * jax.random.normal(jax.random.fold_in(_tk, 500 + 13), (12500, 64), jnp.float32)
        tbl_14 = 0.05 * jax.random.normal(jax.random.fold_in(_tk, 500 + 14), (1000, 64), jnp.float32)
        tbl_15 = 0.05 * jax.random.normal(jax.random.fold_in(_tk, 500 + 15), (12500, 64), jnp.float32)
        tbl_16 = 0.05 * jax.random.normal(jax.random.fold_in(_tk, 500 + 16), (1250, 64), jnp.float32)
        tbl_17 = 0.05 * jax.random.normal(jax.random.fold_in(_tk, 500 + 17), (1250, 64), jnp.float32)
        tbl_18 = 0.05 * jax.random.normal(jax.random.fold_in(_tk, 500 + 18), (1000, 64), jnp.float32)
        tbl_19 = 0.05 * jax.random.normal(jax.random.fold_in(_tk, 500 + 19), (1000, 64), jnp.float32)
        tbl_20 = 0.05 * jax.random.normal(jax.random.fold_in(_tk, 500 + 20), (1250, 64), jnp.float32)
        tbl_21 = 0.05 * jax.random.normal(jax.random.fold_in(_tk, 500 + 21), (12500, 64), jnp.float32)
        tbl_22 = 0.05 * jax.random.normal(jax.random.fold_in(_tk, 500 + 22), (1000, 64), jnp.float32)
        tbl_23 = 0.05 * jax.random.normal(jax.random.fold_in(_tk, 500 + 23), (1000, 64), jnp.float32)
        tbl_24 = 0.05 * jax.random.normal(jax.random.fold_in(_tk, 500 + 24), (1250, 64), jnp.float32)
        tbl_25 = 0.05 * jax.random.normal(jax.random.fold_in(_tk, 500 + 25), (1250, 64), jnp.float32)
        tbl_26 = 0.05 * jax.random.normal(jax.random.fold_in(_tk, 500 + 26), (12500, 64), jnp.float32)
        tbl_27 = 0.05 * jax.random.normal(jax.random.fold_in(_tk, 500 + 27), (1000, 64), jnp.float32)
        tbl_28 = 0.05 * jax.random.normal(jax.random.fold_in(_tk, 500 + 28), (1000, 64), jnp.float32)
        tbl_29 = 0.05 * jax.random.normal(jax.random.fold_in(_tk, 500 + 29), (1250, 64), jnp.float32)
        tbl_30 = 0.05 * jax.random.normal(jax.random.fold_in(_tk, 500 + 30), (1000, 64), jnp.float32)
        tbl_31 = 0.05 * jax.random.normal(jax.random.fold_in(_tk, 500 + 31), (1000, 64), jnp.float32)
        _rk = jax.random.fold_in(_tk, 7)
        W_top1 = 0.0441942 * jax.random.normal(jax.random.fold_in(_tk, 801), (512, 512), jnp.float32)
        W_top2 = 0.0441942 * jax.random.normal(jax.random.fold_in(_tk, 802), (512, 256), jnp.float32)
        W_top3 = 0.0625 * jax.random.normal(jax.random.fold_in(_tk, 803), (256, 1), jnp.float32)
        b_top1 = jnp.zeros((512,), jnp.float32)
        b_top2 = jnp.zeros((256,), jnp.float32)
        return (dense_ctx, ids, tbl_0, tbl_1, tbl_2, tbl_3, tbl_4, tbl_5, tbl_6, tbl_7, tbl_8, tbl_9, tbl_10, tbl_11, tbl_12, tbl_13, tbl_14, tbl_15, tbl_16, tbl_17, tbl_18, tbl_19, tbl_20, tbl_21, tbl_22, tbl_23, tbl_24, tbl_25, tbl_26, tbl_27, tbl_28, tbl_29, tbl_30, tbl_31, W_top1, b_top1, W_top2, b_top2, W_top3)
    dense_ctx, ids, tbl_0, tbl_1, tbl_2, tbl_3, tbl_4, tbl_5, tbl_6, tbl_7, tbl_8, tbl_9, tbl_10, tbl_11, tbl_12, tbl_13, tbl_14, tbl_15, tbl_16, tbl_17, tbl_18, tbl_19, tbl_20, tbl_21, tbl_22, tbl_23, tbl_24, tbl_25, tbl_26, tbl_27, tbl_28, tbl_29, tbl_30, tbl_31, W_top1, b_top1, W_top2, b_top2, W_top3 = _rec_inputs()

    def _L0_rec_setup():
        import jax, jax.numpy as jnp
        import numpy as np
        B = 256
        NUM_FIELDS = 32
        EMBED = 64
        P = NUM_FIELDS * (NUM_FIELDS - 1) // 2
        _ROW, _COL = np.triu_indices(NUM_FIELDS, k=1)
        ROW_IDX = jnp.asarray(_ROW, dtype=jnp.int32)
        COL_IDX = jnp.asarray(_COL, dtype=jnp.int32)
        key = jax.random.key(seed)
        k1, k2 = jax.random.split(key)
        emb_inputs = jax.random.normal(k1, (B, NUM_FIELDS, EMBED), dtype=jnp.float32)
        fan_in = P * EMBED
        fan_out = EMBED
        std = float(np.sqrt(2.0 / (fan_in + fan_out)))
        kernel = jax.random.normal(k2, (EMBED, P, EMBED), dtype=jnp.float32) * std
        return {'emb_inputs': emb_inputs, 'kernel': kernel}
    _L0_rec_all = _L0_rec_setup()
    _L0_rec_in = {k: v for k, v in _L0_rec_all.items() if k in ('kernel',)}
    del _L0_rec_all
    return {'dense_ctx': dense_ctx, 'ids': ids, 'tbl_0': tbl_0, 'tbl_1': tbl_1, 'tbl_2': tbl_2, 'tbl_3': tbl_3, 'tbl_4': tbl_4, 'tbl_5': tbl_5, 'tbl_6': tbl_6, 'tbl_7': tbl_7, 'tbl_8': tbl_8, 'tbl_9': tbl_9, 'tbl_10': tbl_10, 'tbl_11': tbl_11, 'tbl_12': tbl_12, 'tbl_13': tbl_13, 'tbl_14': tbl_14, 'tbl_15': tbl_15, 'tbl_16': tbl_16, 'tbl_17': tbl_17, 'tbl_18': tbl_18, 'tbl_19': tbl_19, 'tbl_20': tbl_20, 'tbl_21': tbl_21, 'tbl_22': tbl_22, 'tbl_23': tbl_23, 'tbl_24': tbl_24, 'tbl_25': tbl_25, 'tbl_26': tbl_26, 'tbl_27': tbl_27, 'tbl_28': tbl_28, 'tbl_29': tbl_29, 'tbl_30': tbl_30, 'tbl_31': tbl_31, 'W_top1': W_top1, 'b_top1': b_top1, 'W_top2': W_top2, 'b_top2': b_top2, 'W_top3': W_top3, 'L0_rec_kernel': _L0_rec_in['kernel']}

def reference(dense_ctx, ids, tbl_0, tbl_1, tbl_2, tbl_3, tbl_4, tbl_5, tbl_6, tbl_7, tbl_8, tbl_9, tbl_10, tbl_11, tbl_12, tbl_13, tbl_14, tbl_15, tbl_16, tbl_17, tbl_18, tbl_19, tbl_20, tbl_21, tbl_22, tbl_23, tbl_24, tbl_25, tbl_26, tbl_27, tbl_28, tbl_29, tbl_30, tbl_31, W_top1, b_top1, W_top2, b_top2, W_top3, L0_rec_kernel):
    import jax
    import jax.numpy as jnp

    def _L0_rec_ref(emb_inputs, kernel):
        import jax, jax.numpy as jnp
        import numpy as np
        B = 256
        NUM_FIELDS = 32
        EMBED = 64
        P = NUM_FIELDS * (NUM_FIELDS - 1) // 2
        _ROW, _COL = np.triu_indices(NUM_FIELDS, k=1)
        ROW_IDX = jnp.asarray(_ROW, dtype=jnp.int32)
        COL_IDX = jnp.asarray(_COL, dtype=jnp.int32)
        p = emb_inputs[:, ROW_IDX]
        q = emb_inputs[:, COL_IDX]
        return jnp.einsum('bne,hne,bnh->bn', p, kernel, q)
    e = jnp.stack([tbl_0[ids[:, 0]], tbl_1[ids[:, 1]], tbl_2[ids[:, 2]], tbl_3[ids[:, 3]], tbl_4[ids[:, 4]], tbl_5[ids[:, 5]], tbl_6[ids[:, 6]], tbl_7[ids[:, 7]], tbl_8[ids[:, 8]], tbl_9[ids[:, 9]], tbl_10[ids[:, 10]], tbl_11[ids[:, 11]], tbl_12[ids[:, 12]], tbl_13[ids[:, 13]], tbl_14[ids[:, 14]], tbl_15[ids[:, 15]], tbl_16[ids[:, 16]], tbl_17[ids[:, 17]], tbl_18[ids[:, 18]], tbl_19[ids[:, 19]], tbl_20[ids[:, 20]], tbl_21[ids[:, 21]], tbl_22[ids[:, 22]], tbl_23[ids[:, 23]], tbl_24[ids[:, 24]], tbl_25[ids[:, 25]], tbl_26[ids[:, 26]], tbl_27[ids[:, 27]], tbl_28[ids[:, 28]], tbl_29[ids[:, 29]], tbl_30[ids[:, 30]], tbl_31[ids[:, 31]]], axis=1)
    z = _L0_rec_ref(e, L0_rec_kernel)
    z = z.reshape(z.shape[0], -1)
    h = jnp.concatenate([z, dense_ctx], axis=1)
    h = jnp.maximum(h @ W_top1 + b_top1, 0.0)
    h = jnp.maximum(h @ W_top2 + b_top2, 0.0)
    y = h @ W_top3
    return y

_drawn_inputs = setup_inputs


def setup_inputs(seed=0):
    import zlib

    import numpy as np

    out = dict(_drawn_inputs(seed))
    spreads = {'b_top1': (0.0, 0.1), 'b_top2': (0.0, 0.1)}
    factors = {'tbl_0': 8.0,
     'tbl_1': 8.0,
     'tbl_2': 8.0,
     'tbl_3': 8.0,
     'tbl_4': 8.0,
     'tbl_5': 8.0,
     'tbl_6': 8.0,
     'tbl_7': 8.0,
     'tbl_8': 8.0,
     'tbl_9': 8.0,
     'tbl_10': 8.0,
     'tbl_11': 8.0,
     'tbl_12': 8.0,
     'tbl_13': 8.0,
     'tbl_14': 8.0,
     'tbl_15': 8.0,
     'tbl_16': 8.0,
     'tbl_17': 8.0,
     'tbl_18': 8.0,
     'tbl_19': 8.0,
     'tbl_20': 8.0,
     'tbl_21': 8.0,
     'tbl_22': 8.0,
     'tbl_23': 8.0,
     'tbl_24': 8.0,
     'tbl_25': 8.0,
     'tbl_26': 8.0,
     'tbl_27': 8.0,
     'tbl_28': 8.0,
     'tbl_29': 8.0,
     'tbl_30': 8.0,
     'tbl_31': 8.0,
     'L0_rec_kernel': 8.0}
    for name, (base, spread) in spreads.items():
        noise = np.random.default_rng([zlib.crc32(name.encode()), seed]).standard_normal(out[name].shape)
        drawn = base * np.exp(spread * noise) if base else spread * noise
        out[name] = jnp.asarray(drawn.astype(out[name].dtype))
    for name, factor in factors.items():
        out[name] = (out[name] * factor).astype(out[name].dtype)
    return out
```

```python
import numpy as np
import concourse.bass as bass
from concourse import mybir
from contextlib import ExitStack

F32 = mybir.dt.float32
F32R = mybir.dt.float32r
U32 = mybir.dt.uint32
ALU = mybir.AluOpType
ACT = mybir.ActivationFunctionType

B = 2048
F = 32
D = 64
H = D // 2
N1, N2 = 512, 256
CTX = 16
NB = 256
NCH = B // NB
BT = NB // 128
GF = 4
NG = F // GF
NP = F // 2
KCOLS = F * (F - 1) // 2 * D
KPIECE = 1024
NPIECE = KCOLS // KPIECE
NZ = 4
XR, PR, UR, ER, SR = 3, 4, 4, 4, 3
SELW = 64
LEAVES = (4, 3, 2, 1)
FC = 512


def owner_columns():
    at, col = {}, 0
    for i in range(F):
        for g in [i // GF] + list(range(i // GF)):
            n = min(GF, i - GF * g)
            at[i, g] = (col, n)
            col += 2 * n * H
    return at


class Event:
    def __init__(self, kind, pair, leaf):
        self.kind, self.pair, self.leaf = kind, pair, leaf
        self.owners = {"cross": [(0, 0, 4), (1, 1, 4)], "inner": [(0, 0, 2), (1, 1, 3)],
                       "single": [(0, 1, 1)]}[kind]


def event_plan():
    events = []
    for g in range(NG):
        a, b = 2 * g, 2 * g + 1
        cross = [[Event("cross", m, leaf) for leaf in range(g)] for m in (a, b)]
        inner, single = Event("inner", b, g), Event("single", a, g)
        if g == NG - 1:
            events += cross[0] + [single] + cross[1] + [inner]
        elif g == 5:
            events += cross[0] + [inner, single] + cross[1]
        else:
            events += cross[0] + cross[1] + [inner, single]
    d, inner_slot = 0, {}
    for ev in events:
        if ev.kind != "single":
            ev.slot = d
            d += 1
            if ev.kind == "inner":
                inner_slot[ev.leaf] = ev.slot
    for ev in events:
        if ev.kind == "single":
            ev.slot = inner_slot[ev.leaf]
    assert d == NZ * 16
    return events, inner_slot


EVENTS, INNER_SLOT = event_plan()
NE = len(EVENTS)
NBATCH = NE // 2
SLOTS = NZ * 16


def z_place(slot, owner, k):
    return slot // 16, 32 * (2 * (slot % 2) + owner) + 4 * (slot // 2 % 8) + k


Z_LAST = [max(n // 2 for n, ev in enumerate(EVENTS) if ev.slot // 16 == z) for z in range(NZ)]
assert all(EVENTS[2 * b + 2].slot // 16 == z + 1 for z, b in enumerate(Z_LAST[:-1]))

PREFETCH = [("U", 0, 58), ("U", 1, 60), ("U", 2, 65), ("Q", 0, 66), ("Q", 1, 68)]
PREPS = [("U", 3, 0), ("U", 4, 2), ("U", 5, 3), ("Q", 2, 4)]
for _g in range(3, NG):
    PREPS += [("U", 2 * _g, _g * (_g - 1)), ("U", 2 * _g + 1, _g * (_g - 1) + 2), ("Q", _g, _g * (_g - 1) + 4)]
NPREP = len(PREFETCH) + len(PREPS)
ORDER = {(k, n): i for i, (k, n, _) in enumerate(PREFETCH + PREPS)}
SPLITS = {m: e - 2 for k, m, e in PREPS if k == "U" and m > 3}
SPLITS_NEXT = {0: 56, 1: 58, 2: 63, 3: 70}
MLP_AT = [7, 9, 11, 13, 15, 17, 19]
M1, M2 = N1 // 128, N2 // 128
NMLP = M1 + M2 + 1

LAST_EVENT = {m: max(n for n, ev in enumerate(EVENTS) if ev.pair == m) for m in range(NP)}
LAST_LEAF = {g: max(n for n, ev in enumerate(EVENTS) if ev.leaf == g) for g in range(NG)}
FIRST_EVENT = {m: min(n for n, ev in enumerate(EVENTS) if ev.pair == m) for m in range(NP)}
FIRST_LEAF = {g: min(n for n, ev in enumerate(EVENTS) if ev.leaf == g) for g in range(NG)}

KAT = owner_columns()


def pieces_needed(e):
    end = max(KAT[2 * ev.pair + f, ev.leaf][0] + KAT[2 * ev.pair + f, ev.leaf][1] * H + 128
              for ev in EVENTS[:e + 1] for _, f, _ in ev.owners)
    return min(NPIECE, -(-end // KPIECE))


def pieces_at(e):
    before = 0 if e < 0 else pieces_needed(min(e + 3, NE - 1))
    upto = pieces_needed(min(e + 4, NE - 1)) if e < NE - 1 else NPIECE
    return range(before, upto)


def count(chunk, per_chunk, k):
    return chunk * per_chunk + k


def positive(chunk, per_chunk, k):
    return not isinstance(chunk, int) or count(chunk, per_chunk, k) > 0


def dlrm_tower(nc, dense_t, ids, tables, w1, b1, w2, b2, w3, kmat, ident_in, sel_in, out):
    ids_v = ids.rearrange("(c t p) f -> c p t f", t=BT, p=128)
    dense_v = dense_t.rearrange("f (c b) -> c f b", b=NB)
    out_v = out.rearrange("(c b) o -> c o b", b=NB)

    ctx = ExitStack()
    with ctx:
        def sb(name, shape, dt=F32):
            return ctx.enter_context(nc.sbuf_tensor(name, shape, dt))

        def sem(name):
            return ctx.enter_context(nc.semaphore(name))

        split_k = sb("split_k", [128, KCOLS], F32R)
        leaf_q = sb("leaf_q", [128, NG, 2 * NB])
        emb_hl = sb("emb_hl", [128, UR, 2, NB], F32R)
        emb_lh = sb("emb_lh", [128, UR, 2, NB], F32R)
        rows_hl = sb("rows_hl", [128, 2, BT, 2, 2 * D])
        rows = sb("rows", [128, ER, BT, GF, D])
        prod = sb("prod", [128, PR, 2, 2, NB])
        zs = sb("zs", [128, NZ, NB])
        weights = sb("weights", [128, M1 * N1 + M1 * N2])
        h1 = sb("h1", [128, M1, NB])
        sel = sb("sel", [128, len(LEAVES), SELW])
        ident = sb("ident", [128, 128])
        ids_sb = sb("ids_sb", [128, BT, F], U32)
        b1_sb = sb("b1_sb", [128, M1])
        b2_sb = sb("b2_sb", [128, M2])
        w3_sb = sb("w3_sb", [128, M2])
        w1_sb = weights[:, 0:NZ * N1].rearrange("p (z n) -> p z n", z=NZ)
        w2_sb = weights[:, NZ * N1:].rearrange("p (k n) -> p k n", k=M1)
        h2 = zs[:, 0:M2, :]
        y_row = h1[0:1, 0, :]

        tiles = [ctx.enter_context(nc.psum_tensor(f"tile{i}", [128, 2 * FC], F32)) for i in range(XR)]
        zacc = ctx.enter_context(nc.psum_tensor("zacc", [128, FC], F32))
        misc = ctx.enter_context(nc.psum_tensor("misc", [128, FC], F32))

        consts_in = sem("consts_in")
        weights_in = sem("weights_in")
        ids_in = sem("ids_in")
        slot_free = sem("slot_free")
        block_free = sem("block_free")
        row_ready = sem("row_ready")
        gathered = [sem(f"gathered{i}") for i in range(ER)]
        staged = [sem(f"staged{i}") for i in range(SR)]
        k_high = sem("k_high")
        k_low = sem("k_low")
        high_made = sem("high_made")
        low_made = sem("low_made")
        prep_filled = sem("prep_filled")
        prep_kept = sem("prep_kept")
        swapped = [sem(f"swapped{i}") for i in range(UR)]
        tile_done = sem("tile_done")
        mult_done = sem("mult_done")
        selected = sem("selected")
        z_kept = sem("z_kept")
        dense_in = sem("dense_in")
        mlp_filled = sem("mlp_filled")
        mlp_kept = sem("mlp_kept")
        out_stored = sem("out_stored")

        block = ctx.enter_context(nc.Block())

        def staging(p):
            return weights[:, (p % SR) * KPIECE:(p % SR + 1) * KPIECE]

        @block.gpsimd
        def _(pool):
            def load_ids(c):
                pool.dma_start(ids_sb[:], ids_v[c]).then_inc(ids_in, 16)
                pool.wait_ge(ids_in, count(c, 16, 16))

            def gather(c, g):
                prev, pg = (c, g - ER) if g >= ER else (c - 1, g - ER + NG)
                if positive(prev, NP, 2 * pg + 2):
                    pool.wait_ge(low_made, count(prev, NP, 2 * pg + 2))
                if positive(prev, NPREP, ORDER["Q", pg] + 1):
                    pool.wait_ge(prep_filled, count(prev, NPREP, ORDER["Q", pg] + 1))
                pool.sem_inc(slot_free, 1)
                for f in range(GF):
                    for t in range(BT):
                        field = GF * g + f
                        pool.indirect_dma_start(
                            rows[:, g % ER, t, f, :], None, tables[field],
                            bass.IndirectOffsetOnAxis(ap=ids_sb[:, t, field:field + 1], axis=0),
                        ).then_inc(gathered[g % ER], 16)

            def chunk(c, last):
                for g in range(2, NG):
                    gather(c, g)
                if not last:
                    for g in range(NG - ER, NG):
                        pool.wait_ge(gathered[g % ER], count(c, 2 * GF * BT * 16, 2 * GF * BT * 16))
                    load_ids(c + 1)
                    gather(c + 1, 0)
                    gather(c + 1, 1)

            load_ids(0)
            gather(0, 0)
            gather(0, 1)
            chunk(0, False)
            with pool.Fori(1, NCH - 1) as c:
                chunk(c, False)
            chunk(NCH - 1, True)

        @block.sync
        def _(sp):
            def stage(p):
                if positive(0, 0, p - SR + 1):
                    sp.wait_ge(k_low, count(0, 0, p - SR + 1))
                src = kmat[:, p * KPIECE:(p + 1) * KPIECE]
                sp.dma_start(staging(p)[0:D], src).then_inc(staged[p % SR], 16)
                sp.dma_start(staging(p)[D:2 * D], src).then_inc(staged[p % SR], 16)

            def swap(c, m):
                sp.wait_ge(prep_kept, count(c, NPREP, ORDER["U", m] + 1))
                s = m % UR
                sp.dma_start(emb_lh[0:D, s].bitcast(F32), emb_hl[D:2 * D, s].bitcast(F32)).then_inc(swapped[s], 16)
                sp.dma_start(emb_lh[D:2 * D, s].bitcast(F32), emb_hl[0:D, s].bitcast(F32)).then_inc(swapped[s], 16)

            def load_dense(c, z):
                sp.wait_ge(z_kept, count(c, NZ, z + 1))
                sp.sem_inc(block_free, 1)
                for g, slot in INNER_SLOT.items():
                    if slot // 16 == z:
                        row = z_place(slot, 0, 3)[1]
                        sp.dma_start(zs[row:row + 33:32, z, :], dense_v[c, 2 * g:2 * g + 2, :]).then_inc(dense_in, 16)

            def store(c):
                sp.wait_ge(mlp_kept, count(c, NMLP, NMLP))
                sp.sem_inc(row_ready, 1)
                sp.dma_start(out_v[c], y_row).then_inc(out_stored, 16)

            def chunk(c, first, last):
                for e in range(NE):
                    if first:
                        for p in pieces_at(e):
                            if p + SR < NPIECE:
                                stage(p + SR)
                    for kind, m, at in PREPS:
                        if kind == "U" and at == e:
                            swap(c, m)
                    for kind, m, at in PREFETCH:
                        if kind == "U" and at == e and not last:
                            swap(c + 1, m)
                    if e == 1 and not first:
                        load_dense(c - 1, NZ - 1)
                    for z in range(NZ - 1):
                        if e == 2 * Z_LAST[z] + 3:
                            load_dense(c, z)
                    if e == MLP_AT[-1] and not first:
                        store(c - 1)

            for p in range(SR):
                stage(p)
            sp.dma_start(ident[:], ident_in).then_inc(consts_in, 16)
            sp.dma_start(sel[:], sel_in).then_inc(consts_in, 16)
            sp.dma_start(b1_sb[:], b1).then_inc(consts_in, 16)
            sp.dma_start(b2_sb[:], b2).then_inc(consts_in, 16)
            sp.dma_start(w3_sb[:], w3).then_inc(consts_in, 16)
            for p in pieces_at(-1):
                if p + SR < NPIECE:
                    stage(p + SR)
            for m in range(3):
                swap(0, m)
            chunk(0, True, False)
            sp.wait_ge(k_low, NPIECE)
            sp.dma_start(w1_sb, w1).then_inc(weights_in, 16)
            sp.dma_start(w2_sb, w2).then_inc(weights_in, 16)
            with sp.Fori(1, NCH - 1) as c:
                chunk(c, False, False)
            chunk(NCH - 1, False, True)
            load_dense(NCH - 1, NZ - 1)
            store(NCH - 1)
            sp.wait_ge(out_stored, 16 * NCH)

        @block.scalar
        def _(act):
            def k_high_part(p):
                act.wait_ge(staged[p % SR], 32 * (p // SR + 1))
                nc.scalar.copy(split_k[:, p * KPIECE:(p + 1) * KPIECE], staging(p)).then_inc(k_high, 1)

            def high_part(c, m):
                g = m // 2
                act.wait_ge(gathered[g % ER], count(c, 2 * GF * BT * 16, (g // ER + 1) * GF * BT * 16))
                prev, pm = (c, m - 2) if m >= 2 else (c - 1, m - 2 + NP)
                if positive(prev, NPREP, ORDER["U", pm] + 1):
                    act.wait_ge(prep_filled, count(prev, NPREP, ORDER["U", pm] + 1))
                f = GF // 2 * (m % 2)
                nc.scalar.copy(rows_hl[:, m % 2, :, :, 0:D].bitcast(F32R),
                               rows[:, g % ER, :, f:f + 2, :]).then_inc(high_made, 1)

            def keep_prep(c, kind, n):
                act.wait_ge(prep_filled, count(c, NPREP, ORDER[kind, n] + 1))
                if kind == "U":
                    prev, pm = (c, n - UR) if n >= UR else (c - 1, n - UR + NP)
                    if positive(prev, NE, LAST_EVENT[pm] + 1):
                        act.wait_ge(tile_done, count(prev, NE, LAST_EVENT[pm] + 1))
                    nc.scalar.copy(emb_hl[:, n % UR].rearrange("p f b -> p (f b)"), misc[:, :]).then_inc(prep_kept, 1)
                else:
                    if positive(c - 1, NE, LAST_LEAF[n] + 1):
                        act.wait_ge(mult_done, count(c - 1, NE, LAST_LEAF[n] + 1))
                    nc.scalar.copy(leaf_q[:, n], misc[:, :]).then_inc(prep_kept, 1)

            def keep_z(c, z):
                act.wait_ge(selected, count(c, NBATCH, Z_LAST[z] + 1))
                if positive(c, NMLP, 0):
                    act.wait_ge(mlp_filled, count(c, NMLP, 0))
                nc.scalar.copy(zs[:, z, :], zacc[:, 0:NB]).then_inc(z_kept, 1)

            def keep_mlp(c, step):
                act.wait_ge(mlp_filled, count(c, NMLP, step + 1))
                if step < M1:
                    if step == 0:
                        if positive(c, 16, 0):
                            act.wait_ge(out_stored, count(c, 16, 0))
                    nc.scalar.activation(h1[:, step, :], misc[:, 0:NB], ACT.Relu,
                                         bias=b1_sb[:, step:step + 1]).then_inc(mlp_kept, 1)
                elif step < M1 + M2:
                    k = step - M1
                    nc.scalar.activation(h2[:, k, :], misc[:, 0:NB], ACT.Relu,
                                         bias=b2_sb[:, k:k + 1]).then_inc(mlp_kept, 1)
                else:
                    nc.scalar.copy(y_row, misc[0:1, 0:NB]).then_inc(mlp_kept, 1)

            def chunk(c, first, last):
                for e in range(NE):
                    for m, at in SPLITS.items():
                        if at == e:
                            high_part(c, m)
                    for m, at in SPLITS_NEXT.items():
                        if at == e and not last:
                            high_part(c + 1, m)
                    if first:
                        for p in pieces_at(e):
                            k_high_part(p)
                    if e == 1 and not first:
                        keep_z(c - 1, NZ - 1)
                    for z in range(NZ - 1):
                        if e == 2 * Z_LAST[z] + 3:
                            keep_z(c, z)
                    for kind, n, at in PREPS:
                        if at == e:
                            keep_prep(c, kind, n)
                    for kind, n, at in PREFETCH:
                        if at == e and not last:
                            keep_prep(c + 1, kind, n)
                    if e in MLP_AT and not first:
                        keep_mlp(c - 1, MLP_AT.index(e))

            for p in pieces_at(-1):
                k_high_part(p)
            high_part(0, 0)
            high_part(0, 1)
            keep_prep(0, "U", 0)
            high_part(0, 2)
            keep_prep(0, "U", 1)
            keep_prep(0, "U", 2)
            keep_prep(0, "Q", 0)
            high_part(0, 3)
            keep_prep(0, "Q", 1)
            act.wait_ge(consts_in, 16 * 5)
            chunk(0, True, False)
            with act.Fori(1, NCH - 1) as c:
                chunk(c, False, False)
            chunk(NCH - 1, False, True)
            keep_z(NCH - 1, NZ - 1)
            for step in range(NMLP):
                keep_mlp(NCH - 1, step)

        @block.vector
        def _(dve):
            def k_low_part(p):
                dve.wait_ge(k_high, p + 1)
                part = split_k[D:2 * D, p * KPIECE:(p + 1) * KPIECE]
                nc.vector.tensor_tensor(part, staging(p)[D:2 * D], part.bitcast(F32),
                                        ALU.subtract).then_inc(k_low, 1)

            def low_part(c, m):
                dve.wait_ge(high_made, count(c, NP, m + 1))
                f = GF // 2 * (m % 2)
                nc.vector.tensor_tensor(rows_hl[:, m % 2, :, :, D:2 * D], rows[:, m // 2 % ER, :, f:f + 2, :],
                                        rows_hl[:, m % 2, :, :, 0:D], ALU.subtract).then_inc(low_made, 1)

            def multiply(c, e):
                ev = EVENTS[e]
                n = len(ev.owners)
                if e == FIRST_LEAF[ev.leaf]:
                    dve.wait_ge(prep_kept, count(c, NPREP, ORDER["Q", ev.leaf] + 1))
                if positive(c, NBATCH, (e - PR) // 2 + 1):
                    dve.wait_ge(selected, count(c, NBATCH, (e - PR) // 2 + 1))
                dve.wait_ge(tile_done, count(c, NE, e + 1))
                leaf = leaf_q[:, ev.leaf:ev.leaf + 1, :]
                nc.vector.tensor_tensor(
                    prod[:, e % PR, 0:n].rearrange("p o h b -> p o (h b)"),
                    tiles[e % XR][:, 0:n * FC].rearrange("p (o x) -> p o x", o=n),
                    leaf.to_broadcast([128, n, 2 * NB]) if n > 1 else leaf,
                    ALU.mult).then_inc(mult_done, 1)

            def chunk(c, first, last):
                for e in range(NE):
                    multiply(c, e)
                    for m, at in SPLITS.items():
                        if at == e:
                            low_part(c, m)
                    for m, at in SPLITS_NEXT.items():
                        if at == e and not last:
                            low_part(c + 1, m)
                    if first:
                        for p in pieces_at(e):
                            k_low_part(p)

            for p in pieces_at(-1):
                k_low_part(p)
            for m in range(4):
                low_part(0, m)
            chunk(0, True, False)
            with dve.Fori(1, NCH - 1) as c:
                chunk(c, False, False)
            chunk(NCH - 1, False, True)

        @block.tensor
        def _(pe):
            def bilinear(c, e, first):
                ev = EVENTS[e]
                if e == FIRST_EVENT[ev.pair] or ev.kind == "single":
                    pe.wait_ge(prep_kept, count(c, NPREP, ORDER["U", ev.pair] + 1))
                    if positive(c, 32 * NP // UR, 32 * (ev.pair // UR + 1)):
                        pe.wait_ge(swapped[ev.pair % UR], count(c, 32 * NP // UR, 32 * (ev.pair // UR + 1)))
                if first:
                    pe.wait_ge(k_low, pieces_needed(e))
                if positive(c, NE, e - XR + 1):
                    pe.wait_ge(mult_done, count(c, NE, e - XR + 1))
                for o, f, _ in ev.owners:
                    col, n = KAT[2 * ev.pair + f, ev.leaf]
                    for half in range(2):
                        at = col + half * n * H
                        dst = tiles[e % XR][:, o * FC + half * NB:o * FC + (half + 1) * NB]
                        nc.tensor.matmul(dst, split_k[:, at:at + 128], emb_hl[:, ev.pair % UR, f, :],
                                         start=True, stop=False)
                        last = nc.tensor.matmul(dst, split_k[:, at:at + 128], emb_lh[:, ev.pair % UR, f, :],
                                                start=False, stop=True)
                last.then_inc(tile_done, 1)

            def select(c, b):
                pair = [2 * b, 2 * b + 1]
                z = EVENTS[pair[0]].slot // 16
                pe.wait_ge(mult_done, count(c, NE, 2 * b + 2))
                if b == (Z_LAST[z - 1] + 1 if z else 0):
                    if positive(c, NZ, z):
                        pe.wait_ge(z_kept, count(c, NZ, z))
                todo = []
                for half in range(2):
                    for e in pair:
                        ev = EVENTS[e]
                        for o, _, live in ev.owners:
                            todo.append((half, e, o, live))
                for half, e, o, live in todo:
                    ev = EVENTS[e]
                    strip = z_place(ev.slot, o, 0)[1] // 32
                    row = 4 * (ev.slot // 2 % 8) + (2 if ev.kind == "single" else 0)
                    use = [(n, h, oo) for n, x in enumerate(EVENTS) for h in range(2) for oo, _, _ in x.owners
                           if x.slot // 16 == z and z_place(x.slot, oo, 0)[1] // 32 == strip]
                    key = lambda t: (t[0] // 2, t[1], t[0], t[2])
                    first, final = min(use, key=key), max(use, key=key)
                    last = nc.tensor.matmul(
                        zacc[32 * strip:32 * strip + 32, 0:NB],
                        sel[:, LEAVES.index(live), 32 - row:64 - row], prod[:, e % PR, o, half, :],
                        start=(e, half, o) == first, stop=(e, half, o) == final)
                last.then_inc(selected, 1)

            def prepare(c, kind, n):
                if positive(c, NPREP, ORDER[kind, n]):
                    pe.wait_ge(prep_kept, count(c, NPREP, ORDER[kind, n]))
                if kind == "U":
                    pe.wait_ge(low_made, count(c, NP, n + 1))
                    for f in range(2):
                        for t in range(BT):
                            at = f * NB + t * 128
                            last = nc.tensor.transpose(misc[:, at:at + 128], rows_hl[:, n % 2, t, f, :], ident[:])
                else:
                    pe.wait_ge(gathered[n % ER], count(c, 2 * GF * BT * 16, (n // ER + 1) * GF * BT * 16))
                    for half in range(2):
                        for t in range(BT):
                            at = half * NB + t * 128
                            last = nc.tensor.transpose(misc[:, at:at + 128],
                                                       rows[:, n % ER, t].rearrange("p f d -> p (f d)")[:, half::2],
                                                       ident[:])
                last.then_inc(prep_filled, 1)

            def perceptron(c, step):
                if positive(c, NMLP, step):
                    pe.wait_ge(mlp_kept, count(c, NMLP, step))
                if step < M1:
                    if step == 0:
                        pe.wait_ge(weights_in, 32)
                        pe.wait_ge(z_kept, count(c, NZ, NZ))
                        pe.wait_ge(dense_in, count(c, 16 * NG, 16 * NG))
                    for z in range(NZ):
                        last = nc.tensor.matmul(misc[:, 0:NB], w1_sb[:, z, step * 128:(step + 1) * 128],
                                                zs[:, z, :], start=(z == 0), stop=(z == NZ - 1))
                elif step < M1 + M2:
                    n = step - M1
                    for k in range(M1):
                        last = nc.tensor.matmul(misc[:, 0:NB], w2_sb[:, k, n * 128:(n + 1) * 128],
                                                h1[:, k, :], start=(k == 0), stop=(k == M1 - 1))
                else:
                    for k in range(M2):
                        last = nc.tensor.matmul(misc[0:1, 0:NB], w3_sb[:, k:k + 1], h2[:, k, :],
                                                start=(k == 0), stop=(k == M2 - 1))
                last.then_inc(mlp_filled, 1)

            def chunk(c, first, last):
                for e in range(NE):
                    bilinear(c, e, first)
                    if e == 1 and not first:
                        select(c - 1, NBATCH - 1)
                    if e % 2 and e >= 3:
                        select(c, (e - 3) // 2)
                    for kind, n, at in PREPS:
                        if at == e:
                            if not first:
                                before = sum(x < e for x in MLP_AT)
                                if positive(c - 1, NMLP, before):
                                    pe.wait_ge(mlp_kept, count(c - 1, NMLP, before))
                            prepare(c, kind, n)
                    for kind, n, at in PREFETCH:
                        if at == e and not last:
                            prepare(c + 1, kind, n)
                    if e in MLP_AT and not first:
                        before = len(PREFETCH) + sum(x <= e for _, _, x in PREPS)
                        if positive(c, NPREP, before):
                            pe.wait_ge(prep_kept, count(c, NPREP, before))
                        perceptron(c - 1, MLP_AT.index(e))

            pe.wait_ge(consts_in, 16 * 5)
            for kind, n, _ in PREFETCH:
                prepare(0, kind, n)
            chunk(0, True, False)
            with pe.Fori(1, NCH - 1) as c:
                chunk(c, False, False)
            chunk(NCH - 1, False, True)
            select(NCH - 1, NBATCH - 1)
            for step in range(NMLP):
                perceptron(NCH - 1, step)


def layouts():
    def pair_number(j, i):
        return j * (2 * F - j - 1) // 2 + i - j - 1

    col_n, col_e = np.zeros(KCOLS, np.int64), np.zeros(KCOLS, np.int64)
    for (i, g), (col, n) in KAT.items():
        for half in range(2):
            for k in range(n):
                at = col + (half * n + k) * H
                col_n[at:at + H] = pair_number(GF * g + k, i)
                col_e[at:at + H] = 2 * np.arange(H) + half
    w1_row = np.full((128, NZ), -1, np.int64)
    for ev in EVENTS:
        for o, f, live in ev.owners:
            for k in range(live):
                z, row = z_place(ev.slot, o, k + (2 if ev.kind == "single" else 0))
                w1_row[row, z] = pair_number(GF * ev.leaf + k, 2 * ev.pair + f)
    for g, slot in INNER_SLOT.items():
        for o in range(2):
            z, row = z_place(slot, o, 3)
            w1_row[row, z] = F * (F - 1) // 2 + 2 * g + o
    assert sorted(w1_row.ravel()) == list(range(N1))
    sel = np.zeros((128, len(LEAVES), SELW), np.float32)
    for n, live in enumerate(LEAVES):
        for p in range(live * H):
            sel[p, n, 32 + p // H] = 1.0
    return col_n, col_e, w1_row, sel


def kernel(**inputs):
    import concourse.bacc as _bacc
    from concourse.bass_utils import run_bass_kernel_spmd as _run

    col_n, col_e, w1_row, sel = layouts()
    get = lambda name: np.asarray(inputs[name])
    arrays = {
        "dense_t": np.ascontiguousarray(get("dense_ctx").T),
        "ids": np.ascontiguousarray(get("ids")),
        "w1": np.ascontiguousarray(get("W_top1")[w1_row]),
        "b1": np.ascontiguousarray(get("b_top1").reshape(M1, 128).T),
        "w2": np.ascontiguousarray(get("W_top2").reshape(M1, 128, N2).transpose(1, 0, 2)),
        "b2": np.ascontiguousarray(get("b_top2").reshape(M2, 128).T),
        "w3": np.ascontiguousarray(get("W_top3").reshape(M2, 128).T),
        "kmat": np.ascontiguousarray(get("L0_rec_kernel")[:, col_n, col_e]),
        "ident": np.eye(128, dtype=np.float32),
        "sel": sel,
    }
    for f in range(F):
        arrays[f"tbl_{f}"] = np.ascontiguousarray(get(f"tbl_{f}"))
    nc = _bacc.Bacc("TRN2", target_bir_lowering=False, num_devices=1)
    aps = {}
    for name, a in arrays.items():
        dt = U32 if name == "ids" else mybir.dt.from_np(a.dtype)
        aps[name] = nc.dram_tensor("in_" + name, a.shape, dt, kind="ExternalInput").ap()
    arrays["ids"] = arrays["ids"].view(np.uint32)
    out = nc.dram_tensor("out", (B, 1), F32, kind="ExternalOutput").ap()
    dlrm_tower(nc, aps["dense_t"], aps["ids"], [aps[f"tbl_{f}"] for f in range(F)], aps["w1"], aps["b1"],
               aps["w2"], aps["b2"], aps["w3"], aps["kmat"], aps["ident"], aps["sel"], out)
    r = _run(nc, [{"in_" + name: a for name, a in arrays.items()}], core_ids=[0])
    return r.results[0]["out"]
```

```python
import numpy as np
import concourse.bass as bass
from concourse import mybir
from contextlib import ExitStack

F32 = mybir.dt.float32
F32R = mybir.dt.float32r
U32 = mybir.dt.uint32
ALU = mybir.AluOpType
ACT = mybir.ActivationFunctionType

B = 2048
F = 32
D = 64
H = D // 2
N1, N2 = 512, 256
CTX = 16
NB = 256
NCH = B // NB
BT = NB // 128
GF = 4
NG = F // GF
NP = F // 2
KCOLS = F * (F - 1) // 2 * D
KPIECE = 1024
NPIECE = KCOLS // KPIECE
POOL_PIECES = range(14, 19)
NZ = 4
XR, PR, UR, ER, SR, WR = 3, 6, 4, 4, 2, 2
LAG = 5
FOLD_EVERY = 2
SELW = 64
LEAVES = (4, 3, 2, 1)
FC = 512


def owner_columns():
    at, col = {}, 0
    for i in range(F):
        for g in [i // GF] + list(range(i // GF)):
            n = min(GF, i - GF * g)
            at[i, g] = (col, n)
            col += 2 * n * H
    return at


class Event:
    def __init__(self, kind, pair, leaf):
        self.kind, self.pair, self.leaf = kind, pair, leaf
        self.owners = {"cross": [(0, 0, 4), (1, 1, 4)], "inner": [(0, 0, 2), (1, 1, 3)],
                       "single": [(0, 1, 1)]}[kind]


def event_plan():
    events = []
    for g in range(NG):
        a, b = 2 * g, 2 * g + 1
        cross = [[Event("cross", m, leaf) for leaf in range(g)] for m in (a, b)]
        inner, single = Event("inner", b, g), Event("single", a, g)
        if g == NG - 1:
            events += cross[0] + [single] + cross[1] + [inner]
        elif g == 5:
            events += cross[0] + [inner, single] + cross[1]
        else:
            events += cross[0] + cross[1] + [inner, single]
    d, inner_slot = 0, {}
    for ev in events:
        if ev.kind != "single":
            ev.slot = d
            d += 1
            if ev.kind == "inner":
                inner_slot[ev.leaf] = ev.slot
    for ev in events:
        if ev.kind == "single":
            ev.slot = inner_slot[ev.leaf]
    assert d == NZ * 16
    return events, inner_slot


EVENTS, INNER_SLOT = event_plan()
NE = len(EVENTS)
NBATCH = NE // 2
SLOTS = NZ * 16


def z_place(slot, owner, k):
    return slot // 16, 32 * (2 * (slot % 2) + owner) + 4 * (slot // 2 % 8) + k


Z_LAST = [max(n // 2 for n, ev in enumerate(EVENTS) if ev.slot // 16 == z) for z in range(NZ)]
assert all(EVENTS[2 * b + 2].slot // 16 == z + 1 for z, b in enumerate(Z_LAST[:-1]))

PREFETCH = [("U", 0, 58), ("U", 1, 60), ("U", 2, 65), ("Q", 0, 66), ("Q", 1, 68)]
PREPS = [("U", 3, 0), ("U", 4, 2), ("U", 5, 3), ("Q", 2, 4)]
for _g in range(3, NG):
    PREPS += [("U", 2 * _g, _g * (_g - 1)), ("U", 2 * _g + 1, _g * (_g - 1) + 2), ("Q", _g, _g * (_g - 1) + 4)]
NPREP = len(PREFETCH) + len(PREPS)
ORDER = {(k, n): i for i, (k, n, _) in enumerate(PREFETCH + PREPS)}
SPLITS = {m: e - 2 for k, m, e in PREPS if k == "U" and m > 3}
SPLITS_NEXT = {0: 56, 1: 58, 2: 63, 3: 70}
MLP_AT = [7, 9, 11, 13, 15, 17, 19]
TAIL_WEIGHTS_AT = 50
WEIGHTS_AT = [1, 3, 8, 10, 12, 14]
M1, M2 = N1 // 128, N2 // 128
NMLP = M1 + M2 + 1

FOLDED = [b for b in range(NBATCH - LAG // 2) if b % FOLD_EVERY == FOLD_EVERY - 1
          and all(ev.kind == "cross" for ev in EVENTS[2 * b:2 * b + 2])]
NFOLD = len(FOLDED)

LAST_EVENT = {m: max(n for n, ev in enumerate(EVENTS) if ev.pair == m) for m in range(NP)}
LAST_LEAF = {g: max(n for n, ev in enumerate(EVENTS) if ev.leaf == g) for g in range(NG)}
FIRST_EVENT = {m: min(n for n, ev in enumerate(EVENTS) if ev.pair == m) for m in range(NP)}
FIRST_LEAF = {g: min(n for n, ev in enumerate(EVENTS) if ev.leaf == g) for g in range(NG)}

KAT = owner_columns()


def pieces_needed(e):
    end = max(KAT[2 * ev.pair + f, ev.leaf][0] + KAT[2 * ev.pair + f, ev.leaf][1] * H + 128
              for ev in EVENTS[:e + 1] for _, f, _ in ev.owners)
    return min(NPIECE, -(-end // KPIECE))


def pieces_at(e):
    before = 0 if e < 0 else pieces_needed(min(e + 3, NE - 1))
    upto = pieces_needed(min(e + 4, NE - 1)) if e < NE - 1 else NPIECE
    return range(before, upto)


def pool_pieces(n):
    return sum(p < n for p in POOL_PIECES)


def count(chunk, per_chunk, k):
    return chunk * per_chunk + k


def positive(chunk, per_chunk, k):
    return not isinstance(chunk, int) or count(chunk, per_chunk, k) > 0


def dlrm_tower(nc, dense_t, ids, tables, w1, b1, w2, b2, w3, kmat, ident_in, sel_in, out):
    ids_v = ids.rearrange("(c t p) f -> c p t f", t=BT, p=128)
    dense_v = dense_t.rearrange("f (c b) -> c f b", b=NB)
    out_v = out.rearrange("(c b) o -> c o b", b=NB)

    ctx = ExitStack()
    with ctx:
        def sb(name, shape, dt=F32):
            return ctx.enter_context(nc.sbuf_tensor(name, shape, dt))

        def sem(name):
            return ctx.enter_context(nc.semaphore(name))

        split_k = sb("split_k", [128, KCOLS], F32R)
        leaf_q = sb("leaf_q", [128, NG, 2 * NB])
        emb_hl = sb("emb_hl", [128, UR, 2, NB], F32R)
        emb_lh = sb("emb_lh", [128, UR, 2, NB], F32R)
        rows_hl = sb("rows_hl", [128, 2, BT, 2, 2 * D])
        rows = sb("rows", [128, ER, BT, GF, D])
        prod = sb("prod", [128, PR, 2, 2, NB])
        zs = sb("zs", [128, NZ, NB])
        spare = sb("spare", [128, SR * KPIECE])
        weights = spare[:, 0:WR * NZ * 128].rearrange("p (r k n) -> p r k n", r=WR, k=NZ)
        h1 = spare[:, WR * NZ * 128:].rearrange("p (m b) -> p m b", m=M1)
        sel = sb("sel", [128, len(LEAVES), SELW])
        ident = sb("ident", [128, 128])
        ids_sb = sb("ids_sb", [128, BT, F], U32)
        b1_sb = sb("b1_sb", [128, M1])
        b2_sb = sb("b2_sb", [128, M2])
        w3_sb = sb("w3_sb", [128, M2])
        h2 = zs[:, 0:M2, :]
        y_row = h1[0:1, 0, :]

        tiles = [ctx.enter_context(nc.psum_tensor(f"tile{i}", [128, 2 * FC], F32)) for i in range(XR)]
        zacc = ctx.enter_context(nc.psum_tensor("zacc", [128, FC], F32))
        misc = ctx.enter_context(nc.psum_tensor("misc", [128, FC], F32))

        consts_in = sem("consts_in")
        weights_in = [sem(f"weights_in{i}") for i in range(WR)]
        ids_in = sem("ids_in")
        slot_free = sem("slot_free")
        block_free = sem("block_free")
        row_ready = sem("row_ready")
        gathered = [sem(f"gathered{i}") for i in range(ER)]
        staged = [sem(f"staged{i}") for i in range(SR)]
        k_high = sem("k_high")
        k_low = sem("k_low")
        k_low_pool = sem("k_low_pool")
        high_made = sem("high_made")
        low_made = sem("low_made")
        prep_filled = sem("prep_filled")
        prep_kept = sem("prep_kept")
        swapped = [sem(f"swapped{i}") for i in range(UR)]
        tile_done = sem("tile_done")
        mult_done = sem("mult_done")
        folded = sem("folded")
        selected = sem("selected")
        z_kept = sem("z_kept")
        dense_in = sem("dense_in")
        tail_weights_in = sem("tail_weights_in")
        mlp_filled = sem("mlp_filled")
        mlp_kept = sem("mlp_kept")
        out_stored = sem("out_stored")

        block = ctx.enter_context(nc.Block())

        def staging(p):
            return spare[:, (p % SR) * KPIECE:(p % SR + 1) * KPIECE]

        def tail_bank(step):
            return [tiles[0][:, 0:FC], tiles[0][:, FC:], tiles[1][:, 0:FC], tiles[1][:, FC:],
                    misc[:, :], zacc[:, :], tiles[2][:, 0:FC]][step]

        def tail_weights(step):
            place = rows[:, step].rearrange("p t f d -> p (t f d)") if step < ER \
                else rows_hl[:, step - ER].rearrange("p t f d -> p (t f d)")
            return place.rearrange("p (k n) -> p k n", k=NZ)

        @block.gpsimd
        def _(pool):
            def load_ids(c):
                pool.dma_start(ids_sb[:], ids_v[c]).then_inc(ids_in, 16)
                pool.wait_ge(ids_in, count(c, 16, 16))

            def gather(c, g):
                prev, pg = (c, g - ER) if g >= ER else (c - 1, g - ER + NG)
                if positive(prev, NP, 2 * pg + 2):
                    pool.wait_ge(low_made, count(prev, NP, 2 * pg + 2))
                if positive(prev, NPREP, ORDER["Q", pg] + 1):
                    pool.wait_ge(prep_filled, count(prev, NPREP, ORDER["Q", pg] + 1))
                pool.sem_inc(slot_free, 1)
                for f in range(GF):
                    for t in range(BT):
                        field = GF * g + f
                        pool.indirect_dma_start(
                            rows[:, g % ER, t, f, :], None, tables[field],
                            bass.IndirectOffsetOnAxis(ap=ids_sb[:, t, field:field + 1], axis=0),
                        ).then_inc(gathered[g % ER], 16)

            def k_low_part(p):
                pool.wait_ge(k_high, p + 1)
                part = split_k[D:2 * D, p * KPIECE:(p + 1) * KPIECE]
                nc.gpsimd.tensor_tensor(part, staging(p)[D:2 * D], part.bitcast(F32),
                                        ALU.subtract).then_inc(k_low_pool, 1)

            def chunk(c, first, last):
                for g in range(2, NG):
                    gather(c, g)
                if first:
                    for g in range(NG - ER, NG):
                        pool.wait_ge(gathered[g % ER], 2 * GF * BT * 16)
                    for p in POOL_PIECES:
                        k_low_part(p)
                    pool.wait_ge(k_low_pool, len(POOL_PIECES))
                if not last:
                    for g in range(NG - ER, NG):
                        pool.wait_ge(gathered[g % ER], count(c, 2 * GF * BT * 16, 2 * GF * BT * 16))
                    load_ids(c + 1)
                    gather(c + 1, 0)
                    gather(c + 1, 1)

            load_ids(0)
            gather(0, 0)
            gather(0, 1)
            chunk(0, True, False)
            with pool.Fori(1, NCH - 1) as c:
                chunk(c, False, False)
            chunk(NCH - 1, False, True)

        @block.sync
        def _(sp):
            def stage(p):
                before = p - SR
                if before in POOL_PIECES:
                    sp.wait_ge(k_low_pool, pool_pieces(before + 1))
                elif before >= 0:
                    sp.wait_ge(k_low, before + 1 - pool_pieces(before + 1))
                src = kmat[:, p * KPIECE:(p + 1) * KPIECE]
                sp.dma_start(staging(p)[0:D], src).then_inc(staged[p % SR], 16)
                sp.dma_start(staging(p)[D:2 * D], src).then_inc(staged[p % SR], 16)

            def swap(c, m):
                sp.wait_ge(prep_kept, count(c, NPREP, ORDER["U", m] + 1))
                s = m % UR
                sp.dma_start(emb_lh[0:D, s].bitcast(F32), emb_hl[D:2 * D, s].bitcast(F32)).then_inc(swapped[s], 16)
                sp.dma_start(emb_lh[D:2 * D, s].bitcast(F32), emb_hl[0:D, s].bitcast(F32)).then_inc(swapped[s], 16)

            def load_dense(c, z):
                sp.wait_ge(z_kept, count(c, NZ, z + 1))
                sp.sem_inc(block_free, 1)
                for g, slot in INNER_SLOT.items():
                    if slot // 16 == z:
                        row = z_place(slot, 0, 3)[1]
                        sp.dma_start(zs[row:row + 33:32, z, :], dense_v[c, 2 * g:2 * g + 2, :]).then_inc(dense_in, 16)

            def load_weights(c, step):
                if step >= WR:
                    sp.wait_ge(mlp_filled, count(c, NMLP, step - WR + 1))
                src = w1[step] if step < M1 else w2[step - M1]
                sp.dma_start(weights[:, step % WR], src).then_inc(weights_in[step % WR], 16)

            def store(c):
                sp.wait_ge(mlp_kept, count(c, NMLP, NMLP))
                sp.sem_inc(row_ready, 1)
                sp.dma_start(out_v[c], y_row).then_inc(out_stored, 16)

            def chunk(c, first, last):
                for e in range(NE):
                    if first:
                        for p in pieces_at(e):
                            if p + SR < NPIECE:
                                stage(p + SR)
                    for kind, m, at in PREPS:
                        if kind == "U" and at == e:
                            swap(c, m)
                    for kind, m, at in PREFETCH:
                        if kind == "U" and at == e and not last:
                            swap(c + 1, m)
                    for z in range(NZ):
                        if e == 2 * Z_LAST[z] + LAG:
                            load_dense(c, z)
                        if e == 2 * Z_LAST[z] + LAG - NE and not first:
                            load_dense(c - 1, z)
                    if e == TAIL_WEIGHTS_AT and last:
                        sp.wait_ge(prep_filled, count(c, NPREP, NPREP))
                        for step in range(M1 + M2):
                            src = w1[step] if step < M1 else w2[step - M1]
                            sp.dma_start(tail_weights(step), src).then_inc(tail_weights_in, 16)
                    if e in WEIGHTS_AT and not first:
                        load_weights(c - 1, WEIGHTS_AT.index(e))
                    if e == MLP_AT[-1] and not first:
                        store(c - 1)

            for p in range(SR):
                stage(p)
            sp.dma_start(ident[:], ident_in).then_inc(consts_in, 16)
            sp.dma_start(sel[:], sel_in).then_inc(consts_in, 16)
            sp.dma_start(b1_sb[:], b1).then_inc(consts_in, 16)
            sp.dma_start(b2_sb[:], b2).then_inc(consts_in, 16)
            sp.dma_start(w3_sb[:], w3).then_inc(consts_in, 16)
            for p in pieces_at(-1):
                if p + SR < NPIECE:
                    stage(p + SR)
            for m in range(3):
                swap(0, m)
            chunk(0, True, False)
            sp.wait_ge(k_low, NPIECE - len(POOL_PIECES))
            with sp.Fori(1, NCH - 1) as c:
                chunk(c, False, False)
            chunk(NCH - 1, False, True)
            load_dense(NCH - 1, NZ - 1)
            store(NCH - 1)
            sp.wait_ge(out_stored, 16 * NCH)

        @block.scalar
        def _(act):
            def k_high_part(p):
                act.wait_ge(staged[p % SR], 32 * (p // SR + 1))
                nc.scalar.copy(split_k[:, p * KPIECE:(p + 1) * KPIECE], staging(p)).then_inc(k_high, 1)

            def high_part(c, m):
                g = m // 2
                act.wait_ge(gathered[g % ER], count(c, 2 * GF * BT * 16, (g // ER + 1) * GF * BT * 16))
                prev, pm = (c, m - 2) if m >= 2 else (c - 1, m - 2 + NP)
                if positive(prev, NPREP, ORDER["U", pm] + 1):
                    act.wait_ge(prep_filled, count(prev, NPREP, ORDER["U", pm] + 1))
                f = GF // 2 * (m % 2)
                nc.scalar.copy(rows_hl[:, m % 2, :, :, 0:D].bitcast(F32R),
                               rows[:, g % ER, :, f:f + 2, :]).then_inc(high_made, 1)

            def keep_prep(c, kind, n):
                act.wait_ge(prep_filled, count(c, NPREP, ORDER[kind, n] + 1))
                if kind == "U":
                    prev, pm = (c, n - UR) if n >= UR else (c - 1, n - UR + NP)
                    if positive(prev, NE, LAST_EVENT[pm] + 1):
                        act.wait_ge(tile_done, count(prev, NE, LAST_EVENT[pm] + 1))
                    nc.scalar.copy(emb_hl[:, n % UR].rearrange("p f b -> p (f b)"), misc[:, :]).then_inc(prep_kept, 1)
                else:
                    if positive(c - 1, NE, LAST_LEAF[n] + 1):
                        act.wait_ge(mult_done, count(c - 1, NE, LAST_LEAF[n] + 1))
                    nc.scalar.copy(leaf_q[:, n], misc[:, :]).then_inc(prep_kept, 1)

            def keep_z(c, z):
                act.wait_ge(selected, count(c, NBATCH, Z_LAST[z] + 1))
                if positive(c, NMLP, 0):
                    act.wait_ge(mlp_filled, count(c, NMLP, 0))
                nc.scalar.copy(zs[:, z, :], zacc[:, 0:NB]).then_inc(z_kept, 1)

            def keep_mlp(c, step, bank):
                act.wait_ge(mlp_filled, count(c, NMLP, step + 1))
                if step < M1:
                    if step == 0:
                        if positive(c, 16, 0):
                            act.wait_ge(out_stored, count(c, 16, 0))
                    nc.scalar.activation(h1[:, step, :], bank[:, 0:NB], ACT.Relu,
                                         bias=b1_sb[:, step:step + 1]).then_inc(mlp_kept, 1)
                elif step < M1 + M2:
                    k = step - M1
                    nc.scalar.activation(h2[:, k, :], bank[:, 0:NB], ACT.Relu,
                                         bias=b2_sb[:, k:k + 1]).then_inc(mlp_kept, 1)
                else:
                    nc.scalar.copy(y_row, bank[0:1, 0:NB]).then_inc(mlp_kept, 1)

            def chunk(c, first, last):
                for e in range(NE):
                    for m, at in SPLITS.items():
                        if at == e:
                            high_part(c, m)
                    for m, at in SPLITS_NEXT.items():
                        if at == e and not last:
                            high_part(c + 1, m)
                    if first:
                        for p in pieces_at(e):
                            k_high_part(p)
                    for z in range(NZ):
                        if e == 2 * Z_LAST[z] + LAG:
                            keep_z(c, z)
                        if e == 2 * Z_LAST[z] + LAG - NE and not first:
                            keep_z(c - 1, z)
                    for kind, n, at in PREPS:
                        if at == e:
                            keep_prep(c, kind, n)
                    for kind, n, at in PREFETCH:
                        if at == e and not last:
                            keep_prep(c + 1, kind, n)
                    if e in MLP_AT and not first:
                        keep_mlp(c - 1, MLP_AT.index(e), misc[:, :])

            for p in pieces_at(-1):
                k_high_part(p)
            high_part(0, 0)
            high_part(0, 1)
            keep_prep(0, "U", 0)
            high_part(0, 2)
            keep_prep(0, "U", 1)
            keep_prep(0, "U", 2)
            keep_prep(0, "Q", 0)
            high_part(0, 3)
            keep_prep(0, "Q", 1)
            act.wait_ge(consts_in, 16 * 5)
            chunk(0, True, False)
            with act.Fori(1, NCH - 1) as c:
                chunk(c, False, False)
            chunk(NCH - 1, False, True)
            keep_z(NCH - 1, NZ - 1)
            for step in range(NMLP):
                keep_mlp(NCH - 1, step, tail_bank(step))

        @block.vector
        def _(dve):
            def k_low_part(p):
                dve.wait_ge(k_high, p + 1)
                part = split_k[D:2 * D, p * KPIECE:(p + 1) * KPIECE]
                nc.vector.tensor_tensor(part, staging(p)[D:2 * D], part.bitcast(F32),
                                        ALU.subtract).then_inc(k_low, 1)

            def low_part(c, m):
                dve.wait_ge(high_made, count(c, NP, m + 1))
                f = GF // 2 * (m % 2)
                nc.vector.tensor_tensor(rows_hl[:, m % 2, :, :, D:2 * D], rows[:, m // 2 % ER, :, f:f + 2, :],
                                        rows_hl[:, m % 2, :, :, 0:D], ALU.subtract).then_inc(low_made, 1)

            def multiply(c, e):
                ev = EVENTS[e]
                n = len(ev.owners)
                if e == FIRST_LEAF[ev.leaf]:
                    dve.wait_ge(prep_kept, count(c, NPREP, ORDER["Q", ev.leaf] + 1))
                if positive(c, NBATCH, (e - PR) // 2 + 1):
                    dve.wait_ge(selected, count(c, NBATCH, (e - PR) // 2 + 1))
                dve.wait_ge(tile_done, count(c, NE, e + 1))
                leaf = leaf_q[:, ev.leaf:ev.leaf + 1, :]
                nc.vector.tensor_tensor(
                    prod[:, e % PR, 0:n].rearrange("p o h b -> p o (h b)"),
                    tiles[e % XR][:, 0:n * FC].rearrange("p (o x) -> p o x", o=n),
                    leaf.to_broadcast([128, n, 2 * NB]) if n > 1 else leaf,
                    ALU.mult).then_inc(mult_done, 1)

            def fold(c, b):
                dve.wait_ge(mult_done, count(c, NE, 2 * b + 2))
                s = 2 * b % PR
                nc.vector.tensor_tensor(prod[:, s:s + 2, :, 0], prod[:, s:s + 2, :, 0], prod[:, s:s + 2, :, 1],
                                        ALU.add).then_inc(folded, 1)

            def chunk(c, first, last):
                for e in range(NE):
                    multiply(c, e)
                    if e // 2 in FOLDED and e % 2 and not first:
                        fold(c, e // 2)
                    for m, at in SPLITS.items():
                        if at == e:
                            low_part(c, m)
                    for m, at in SPLITS_NEXT.items():
                        if at == e and not last:
                            low_part(c + 1, m)
                    if first:
                        for p in pieces_at(e):
                            if p not in POOL_PIECES:
                                k_low_part(p)

            for p in pieces_at(-1):
                k_low_part(p)
            for m in range(4):
                low_part(0, m)
            chunk(0, True, False)
            with dve.Fori(1, NCH - 1) as c:
                chunk(c, False, False)
            chunk(NCH - 1, False, True)

        @block.tensor
        def _(pe):
            def bilinear(c, e, first):
                ev = EVENTS[e]
                if e == FIRST_EVENT[ev.pair] or ev.kind == "single":
                    pe.wait_ge(prep_kept, count(c, NPREP, ORDER["U", ev.pair] + 1))
                    if positive(c, 32 * NP // UR, 32 * (ev.pair // UR + 1)):
                        pe.wait_ge(swapped[ev.pair % UR], count(c, 32 * NP // UR, 32 * (ev.pair // UR + 1)))
                if first:
                    n = pool_pieces(pieces_needed(e))
                    pe.wait_ge(k_low, pieces_needed(e) - n)
                    if n:
                        pe.wait_ge(k_low_pool, n)
                if positive(c, NE, e - XR + 1):
                    pe.wait_ge(mult_done, count(c, NE, e - XR + 1))
                for o, f, _ in ev.owners:
                    col, n = KAT[2 * ev.pair + f, ev.leaf]
                    for half in range(2):
                        at = col + half * n * H
                        dst = tiles[e % XR][:, o * FC + half * NB:o * FC + (half + 1) * NB]
                        nc.tensor.matmul(dst, split_k[:, at:at + 128], emb_hl[:, ev.pair % UR, f, :],
                                         start=True, stop=False)
                        last = nc.tensor.matmul(dst, split_k[:, at:at + 128], emb_lh[:, ev.pair % UR, f, :],
                                                start=False, stop=True)
                last.then_inc(tile_done, 1)

            def select(c, b, folds=True):
                pair = [2 * b, 2 * b + 1]
                z = EVENTS[pair[0]].slot // 16
                pe.wait_ge(mult_done, count(c, NE, 2 * b + 2))
                if b == (Z_LAST[z - 1] + 1 if z else 0):
                    if positive(c, NZ, z):
                        pe.wait_ge(z_kept, count(c, NZ, z))
                halves = 2
                if b in FOLDED and folds:
                    halves = 1
                    pe.wait_ge(folded, count(c - 1, NFOLD, FOLDED.index(b) + 1))
                todo = []
                for half in range(halves):
                    for e in pair:
                        ev = EVENTS[e]
                        for o, _, live in ev.owners:
                            todo.append((half, e, o, live))
                for half, e, o, live in todo:
                    ev = EVENTS[e]
                    strip = z_place(ev.slot, o, 0)[1] // 32
                    row = 4 * (ev.slot // 2 % 8) + (2 if ev.kind == "single" else 0)
                    use = [(n, h, oo) for n, x in enumerate(EVENTS) for h in range(1 if n // 2 in FOLDED and folds else 2) for oo, _, _ in x.owners
                           if x.slot // 16 == z and z_place(x.slot, oo, 0)[1] // 32 == strip]
                    key = lambda t: (t[0] // 2, t[1], t[0], t[2])
                    first, final = min(use, key=key), max(use, key=key)
                    last = nc.tensor.matmul(
                        zacc[32 * strip:32 * strip + 32, 0:NB],
                        sel[:, LEAVES.index(live), 32 - row:64 - row], prod[:, e % PR, o, half, :],
                        start=(e, half, o) == first, stop=(e, half, o) == final)
                last.then_inc(selected, 1)

            def prepare(c, kind, n):
                if positive(c, NPREP, ORDER[kind, n]):
                    pe.wait_ge(prep_kept, count(c, NPREP, ORDER[kind, n]))
                if kind == "U":
                    pe.wait_ge(low_made, count(c, NP, n + 1))
                    for f in range(2):
                        for t in range(BT):
                            at = f * NB + t * 128
                            last = nc.tensor.transpose(misc[:, at:at + 128], rows_hl[:, n % 2, t, f, :], ident[:])
                else:
                    pe.wait_ge(gathered[n % ER], count(c, 2 * GF * BT * 16, (n // ER + 1) * GF * BT * 16))
                    for half in range(2):
                        for t in range(BT):
                            at = half * NB + t * 128
                            last = nc.tensor.transpose(misc[:, at:at + 128],
                                                       rows[:, n % ER, t].rearrange("p f d -> p (f d)")[:, half::2],
                                                       ident[:])
                last.then_inc(prep_filled, 1)

            def perceptron(c, step):
                if positive(c, NMLP, step):
                    pe.wait_ge(mlp_kept, count(c, NMLP, step))
                if step < M1 + M2:
                    uses = (M1 + M2) // WR
                    pe.wait_ge(weights_in[step % WR], count(c, 16 * uses, 16 * (step // WR + 1)))
                if step < M1:
                    if step == 0:
                        pe.wait_ge(z_kept, count(c, NZ, NZ))
                        pe.wait_ge(dense_in, count(c, 16 * NG, 16 * NG))
                    for z in range(NZ):
                        last = nc.tensor.matmul(misc[:, 0:NB], weights[:, step % WR, z, :],
                                                zs[:, z, :], start=(z == 0), stop=(z == NZ - 1))
                elif step < M1 + M2:
                    for k in range(M1):
                        last = nc.tensor.matmul(misc[:, 0:NB], weights[:, step % WR, k, :],
                                                h1[:, k, :], start=(k == 0), stop=(k == M1 - 1))
                else:
                    for k in range(M2):
                        last = nc.tensor.matmul(misc[0:1, 0:NB], w3_sb[:, k:k + 1], h2[:, k, :],
                                                start=(k == 0), stop=(k == M2 - 1))
                last.then_inc(mlp_filled, 1)

            def chunk(c, first, last):
                for e in range(NE):
                    bilinear(c, e, first)
                    if e % 2 and e >= LAG:
                        select(c, (e - LAG) // 2, not first)
                    elif e % 2 and not first:
                        select(c - 1, (e - LAG) // 2 + NBATCH)
                    for kind, n, at in PREPS:
                        if at == e:
                            if not first:
                                before = sum(x < e for x in MLP_AT)
                                if positive(c - 1, NMLP, before):
                                    pe.wait_ge(mlp_kept, count(c - 1, NMLP, before))
                            prepare(c, kind, n)
                    for kind, n, at in PREFETCH:
                        if at == e and not last:
                            prepare(c + 1, kind, n)
                    if e in MLP_AT and not first:
                        before = len(PREFETCH) + sum(x <= e for _, _, x in PREPS)
                        if positive(c, NPREP, before):
                            pe.wait_ge(prep_kept, count(c, NPREP, before))
                        perceptron(c - 1, MLP_AT.index(e))

            pe.wait_ge(consts_in, 16 * 5)
            for kind, n, _ in PREFETCH:
                prepare(0, kind, n)
            chunk(0, True, False)
            with pe.Fori(1, NCH - 1) as c:
                chunk(c, False, False)
            chunk(NCH - 1, False, True)
            c, z = NCH - 1, NZ - 1

            def first_layer(step, blocks):
                for k in blocks:
                    last = nc.tensor.matmul(tail_bank(step)[:, 0:NB], tail_weights(step)[:, k, :], zs[:, k, :],
                                            start=(k == 0), stop=(k == z))
                return last

            for b in range(NBATCH - LAG // 2, NBATCH - 1):
                select(c, b)
            pe.wait_ge(tail_weights_in, 16 * (M1 + M2))
            pe.wait_ge(z_kept, count(c, NZ, z))
            pe.wait_ge(dense_in, count(c, 16 * NG, 16 * sum(slot // 16 < z for slot in INNER_SLOT.values())))
            pe.wait_ge(mult_done, count(c, NE, NE - 2))
            first_layer(0, range(z))
            first_layer(1, range(z))
            select(c, NBATCH - 1)
            first_layer(2, range(z))
            first_layer(3, range(z))
            pe.wait_ge(z_kept, count(c, NZ, NZ))
            pe.wait_ge(dense_in, count(c, 16 * NG, 16 * NG))
            for step in range(M1):
                first_layer(step, [z]).then_inc(mlp_filled, 1)
            for step in range(M1, M1 + M2):
                for k in range(M1):
                    pe.wait_ge(mlp_kept, count(c, NMLP, k + 1))
                    last = nc.tensor.matmul(tail_bank(step)[:, 0:NB], tail_weights(step)[:, k, :], h1[:, k, :],
                                            start=(k == 0), stop=(k == M1 - 1))
                last.then_inc(mlp_filled, 1)
            for k in range(M2):
                pe.wait_ge(mlp_kept, count(c, NMLP, M1 + k + 1))
                last = nc.tensor.matmul(tail_bank(NMLP - 1)[0:1, 0:NB], w3_sb[:, k:k + 1], h2[:, k, :],
                                        start=(k == 0), stop=(k == M2 - 1))
            last.then_inc(mlp_filled, 1)


def layouts():
    def pair_number(j, i):
        return j * (2 * F - j - 1) // 2 + i - j - 1

    col_n, col_e = np.zeros(KCOLS, np.int64), np.zeros(KCOLS, np.int64)
    for (i, g), (col, n) in KAT.items():
        for half in range(2):
            for k in range(n):
                at = col + (half * n + k) * H
                col_n[at:at + H] = pair_number(GF * g + k, i)
                col_e[at:at + H] = 2 * np.arange(H) + half
    w1_row = np.full((128, NZ), -1, np.int64)
    for ev in EVENTS:
        for o, f, live in ev.owners:
            for k in range(live):
                z, row = z_place(ev.slot, o, k + (2 if ev.kind == "single" else 0))
                w1_row[row, z] = pair_number(GF * ev.leaf + k, 2 * ev.pair + f)
    for g, slot in INNER_SLOT.items():
        for o in range(2):
            z, row = z_place(slot, o, 3)
            w1_row[row, z] = F * (F - 1) // 2 + 2 * g + o
    assert sorted(w1_row.ravel()) == list(range(N1))
    sel = np.zeros((128, len(LEAVES), SELW), np.float32)
    for n, live in enumerate(LEAVES):
        for p in range(live * H):
            sel[p, n, 32 + p // H] = 1.0
    return col_n, col_e, w1_row, sel


def kernel(**inputs):
    import concourse.bacc as _bacc
    from concourse.bass_utils import run_bass_kernel_spmd as _run

    col_n, col_e, w1_row, sel = layouts()
    get = lambda name: np.asarray(inputs[name])
    arrays = {
        "dense_t": np.ascontiguousarray(get("dense_ctx").T),
        "ids": np.ascontiguousarray(get("ids")),
        "w1": np.ascontiguousarray(get("W_top1")[w1_row].reshape(128, NZ, M1, 128).transpose(2, 0, 1, 3)),
        "b1": np.ascontiguousarray(get("b_top1").reshape(M1, 128).T),
        "w2": np.ascontiguousarray(get("W_top2").reshape(M1, 128, M2, 128).transpose(2, 1, 0, 3)),
        "b2": np.ascontiguousarray(get("b_top2").reshape(M2, 128).T),
        "w3": np.ascontiguousarray(get("W_top3").reshape(M2, 128).T),
        "kmat": np.ascontiguousarray(get("L0_rec_kernel")[:, col_n, col_e]),
        "ident": np.eye(128, dtype=np.float32),
        "sel": sel,
    }
    for f in range(F):
        arrays[f"tbl_{f}"] = np.ascontiguousarray(get(f"tbl_{f}"))
    nc = _bacc.Bacc("TRN2", target_bir_lowering=False, num_devices=1)
    aps = {}
    for name, a in arrays.items():
        dt = U32 if name == "ids" else mybir.dt.from_np(a.dtype)
        aps[name] = nc.dram_tensor("in_" + name, a.shape, dt, kind="ExternalInput").ap()
    arrays["ids"] = arrays["ids"].view(np.uint32)
    out = nc.dram_tensor("out", (B, 1), F32, kind="ExternalOutput").ap()
    dlrm_tower(nc, aps["dense_t"], aps["ids"], [aps[f"tbl_{f}"] for f in range(F)], aps["w1"], aps["b1"],
               aps["w2"], aps["b2"], aps["w3"], aps["kmat"], aps["ident"], aps["sel"], out)
    r = _run(nc, [{"in_" + name: a for name, a in arrays.items()}], core_ids=[0])
    return r.results[0]["out"]
```

```python
import numpy as np
import concourse.bass as bass
from concourse import mybir
from contextlib import ExitStack

F32 = mybir.dt.float32
F32R = mybir.dt.float32r
U32 = mybir.dt.uint32
ALU = mybir.AluOpType
ACT = mybir.ActivationFunctionType

B = 2048
F = 32
D = 64
H = D // 2
N1, N2 = 512, 256
CTX = 16
NB = 256
NCH = B // NB
BT = NB // 128
GF = 4
NG = F // GF
NP = F // 2
KCOLS = F * (F - 1) // 2 * D
KPIECE = 1024
NPIECE = KCOLS // KPIECE
POOL_PIECES = range(14, 19)
NZ = 4
XR, PR, UR, ER, SR, WR = 3, 6, 4, 4, 2, 2
LAG = 5
FOLD_EVERY = 3
YR = 2
SELW = 64
LEAVES = (4, 3, 2, 1)
FC = 512


class Event:
    def __init__(self, kind, pair, leaf):
        self.kind, self.pair, self.leaf = kind, pair, leaf
        self.owners = {"cross": [(0, 0, 4), (1, 1, 4)], "inner": [(0, 0, 2), (1, 1, 3)],
                       "single": [(0, 1, 1)]}[kind]


def event_plan():
    events = []
    for g in range(NG):
        a, b = 2 * g, 2 * g + 1
        cross = [[Event("cross", m, leaf) for leaf in range(g)] for m in (a, b)]
        inner, single = Event("inner", b, g), Event("single", a, g)
        if g == NG - 1:
            events += [cross[0][0], cross[1][0], cross[0][1], cross[1][1]] + cross[0][2:] + [single]
            events += cross[1][2:] + [inner]
        elif g == 5:
            events += cross[0] + [inner, single] + cross[1]
        else:
            events += cross[0] + cross[1] + [inner, single]
    d, inner_slot = 0, {}
    for ev in events:
        if ev.kind != "single":
            ev.slot = d
            d += 1
            if ev.kind == "inner":
                inner_slot[ev.leaf] = ev.slot
    for ev in events:
        if ev.kind == "single":
            ev.slot = inner_slot[ev.leaf]
    assert d == NZ * 16
    return events, inner_slot


EVENTS, INNER_SLOT = event_plan()
NE = len(EVENTS)
NBATCH = NE // 2
SLOTS = NZ * 16


def z_place(slot, owner, k):
    return slot // 16, 32 * (2 * (slot % 2) + owner) + 4 * (slot // 2 % 8) + k


Z_LAST = [max(n // 2 for n, ev in enumerate(EVENTS) if ev.slot // 16 == z) for z in range(NZ)]
assert all(EVENTS[2 * b + 2].slot // 16 == z + 1 for z, b in enumerate(Z_LAST[:-1]))

PREP_AT = {4: 0, 5: 2, 6: 7, 7: 9}
DUP_AT = {3: 0, 4: 2, 5: 3, 6: 7, 7: 10}
LEAF_AT = {4: 2, 5: 4, 6: 8, 7: 10}
for _g in range(4, NG):
    for _k in range(2):
        PREP_AT[2 * _g + _k] = _g * (_g - 1) + 2 * _k
        DUP_AT[2 * _g + _k] = _g * (_g - 1) + 2 * _k + 1
        LEAF_AT[2 * _g + _k] = _g * (_g - 1) + 2 * _k + 2
PREP_NEXT = {0: 57, 1: 59, 2: 64, 3: 67}
DUP_NEXT = {0: 58, 1: 60, 2: 66}
LEAF_NEXT = {0: 59, 1: 61, 2: 65, 3: 68}
MLP_AT = [8, 10, 13, 15, 17, 19, 21]
TAIL_WEIGHTS_AT = 50
WEIGHTS_AT = [1, 1, 8, 10, 13, 15]
M1, M2 = N1 // 128, N2 // 128
NMLP = M1 + M2 + 1

FOLDED = [b for b in range(NBATCH - LAG // 2)
          if MLP_AT[0] // 2 <= b < MLP_AT[-1] // 2 or b % FOLD_EVERY == 0]
NFOLD = len(FOLDED)

LAST_EVENT = {m: max(n for n, ev in enumerate(EVENTS) if ev.pair == m) for m in range(NP)}
LAST_LEAF = {g: max(n for n, ev in enumerate(EVENTS) if ev.leaf == g) for g in range(NG)}
FIRST_EVENT = {m: min(n for n, ev in enumerate(EVENTS) if ev.pair == m) for m in range(NP)}
FIRST_LEAF = {g: min(n for n, ev in enumerate(EVENTS) if ev.leaf == g) for g in range(NG)}

def owner_columns():
    at, col = {}, 0
    for ev in EVENTS[:-2] + [EVENTS[-1], EVENTS[-2]]:
        for _, f, live in ev.owners:
            at[2 * ev.pair + f, ev.leaf] = (col, live)
            col += 2 * live * H
    assert col == KCOLS
    return at


KAT = owner_columns()


def pieces_needed(e):
    end = max(KAT[2 * ev.pair + f, ev.leaf][0] + KAT[2 * ev.pair + f, ev.leaf][1] * H + 128
              for ev in EVENTS[:e + 1] for _, f, _ in ev.owners)
    return min(NPIECE, -(-end // KPIECE))


def pieces_at(e):
    before = 0 if e < 0 else pieces_needed(min(e + 3, NE - 1))
    upto = pieces_needed(min(e + 4, NE - 1)) if e < NE - 1 else NPIECE
    return range(before, upto)


def pool_pieces(n):
    return sum(p < n for p in POOL_PIECES)


def count(chunk, per_chunk, k):
    return chunk * per_chunk + k


def positive(chunk, per_chunk, k):
    return not isinstance(chunk, int) or count(chunk, per_chunk, k) > 0


def dlrm_tower(nc, dense_t, ids, tables, w1, b1, w2, b2, w3, kmat, ident_in, sel_in, out):
    ids_v = ids.rearrange("(c t p) f -> c p t f", t=BT, p=128)
    dense_v = dense_t.rearrange("f (c b) -> c f b", b=NB)
    out_v = out.rearrange("(c b) o -> c o b", b=NB)

    ctx = ExitStack()
    with ctx:
        def sb(name, shape, dt=F32):
            return ctx.enter_context(nc.sbuf_tensor(name, shape, dt))

        def sem(name):
            return ctx.enter_context(nc.semaphore(name))

        split_k = sb("split_k", [128, KCOLS], F32R)
        leaf_q = sb("leaf_q", [128, NG, 2 * NB])
        emb = sb("emb", [128, UR, 2, 2, NB], F32R)
        parts = sb("parts", [128, YR, 2, NB], F32R)
        plain = sb("plain", [128, YR, NB])
        rows = sb("rows", [128, ER, BT, GF, D])
        prod = sb("prod", [128, PR, 2, 2, NB])
        zs = sb("zs", [128, NZ, NB])
        spare = sb("spare", [128, SR * KPIECE])
        weights = spare[:, 0:WR * NZ * 128].rearrange("p (r k n) -> p r k n", r=WR, k=NZ)
        h1 = spare[:, WR * NZ * 128:].rearrange("p (m b) -> p m b", m=M1)
        sel = sb("sel", [128, len(LEAVES), SELW])
        ident = sb("ident", [128, 128])
        ids_sb = sb("ids_sb", [128, BT, F], U32)
        b1_sb = sb("b1_sb", [128, M1])
        b2_sb = sb("b2_sb", [128, M2])
        w3_sb = sb("w3_sb", [128, M2])
        h2 = zs[:, 0:M2, :]
        y_row = h1[0:1, 0, :]

        tiles = [ctx.enter_context(nc.psum_tensor(f"tile{i}", [128, 2 * FC], F32)) for i in range(XR)]
        zacc = ctx.enter_context(nc.psum_tensor("zacc", [128, FC], F32))
        misc = ctx.enter_context(nc.psum_tensor("misc", [128, FC], F32))

        consts_in = sem("consts_in")
        weights_in = [sem(f"weights_in{i}") for i in range(WR)]
        ids_in = sem("ids_in")
        slot_free = sem("slot_free")
        ring_free = sem("ring_free")
        leaves_free = sem("leaves_free")
        block_free = sem("block_free")
        row_ready = sem("row_ready")
        gathered = [sem(f"gathered{i}") for i in range(ER)]
        staged = [sem(f"staged{i}") for i in range(SR)]
        k_high = sem("k_high")
        k_low = sem("k_low")
        k_low_pool = sem("k_low_pool")
        prep_filled = sem("prep_filled")
        high_made = sem("high_made")
        prep_kept = sem("prep_kept")
        low_made = sem("low_made")
        dup_in = [sem(f"dup_in{i}") for i in range(UR)]
        leaf_in = [sem(f"leaf_in{i}") for i in range(YR)]
        tile_done = sem("tile_done")
        mult_done = sem("mult_done")
        folded = sem("folded")
        selected = sem("selected")
        z_kept = sem("z_kept")
        dense_in = sem("dense_in")
        tail_weights_in = sem("tail_weights_in")
        mlp_filled = sem("mlp_filled")
        mlp_kept = sem("mlp_kept")
        out_stored = sem("out_stored")

        block = ctx.enter_context(nc.Block())

        def staging(p):
            return spare[:, (p % SR) * KPIECE:(p % SR + 1) * KPIECE]

        def tail_bank(step):
            return [tiles[0][:, 0:FC], tiles[0][:, FC:], tiles[1][:, 0:FC], tiles[1][:, FC:],
                    misc[:, :], zacc[:, :], tiles[2][:, 0:FC]][step]

        def tail_weights(step):
            place = rows[:, step].rearrange("p t f d -> p (t f d)") if step < ER \
                else parts[:, step - ER].bitcast(F32).rearrange("p x b -> p (x b)")
            return place.rearrange("p (k n) -> p k n", k=NZ)

        @block.gpsimd
        def _(pool):
            def load_ids(c):
                pool.dma_start(ids_sb[:], ids_v[c]).then_inc(ids_in, 16)
                pool.wait_ge(ids_in, count(c, 16, 16))

            def gather(c, g):
                prev, pg = (c, g - ER) if g >= ER else (c - 1, g - ER + NG)
                if positive(prev, NP, 2 * pg + 2):
                    pool.wait_ge(prep_filled, count(prev, NP, 2 * pg + 2))
                pool.sem_inc(slot_free, 1)
                for f in range(GF):
                    for t in range(BT):
                        field = GF * g + f
                        pool.indirect_dma_start(
                            rows[:, g % ER, t, f, :], None, tables[field],
                            bass.IndirectOffsetOnAxis(ap=ids_sb[:, t, field:field + 1], axis=0),
                        ).then_inc(gathered[g % ER], 16)

            def k_low_part(p):
                pool.wait_ge(k_high, p + 1)
                part = split_k[D:2 * D, p * KPIECE:(p + 1) * KPIECE]
                nc.gpsimd.tensor_tensor(part, staging(p)[D:2 * D], part.bitcast(F32),
                                        ALU.subtract).then_inc(k_low_pool, 1)

            def chunk(c, first, last):
                for g in range(2, NG):
                    gather(c, g)
                if first:
                    for g in range(NG - ER, NG):
                        pool.wait_ge(gathered[g % ER], 2 * GF * BT * 16)
                    for p in POOL_PIECES:
                        k_low_part(p)
                    pool.wait_ge(k_low_pool, len(POOL_PIECES))
                if not last:
                    for g in range(NG - ER, NG):
                        pool.wait_ge(gathered[g % ER], count(c, 2 * GF * BT * 16, 2 * GF * BT * 16))
                    load_ids(c + 1)
                    gather(c + 1, 0)
                    gather(c + 1, 1)

            load_ids(0)
            gather(0, 0)
            gather(0, 1)
            chunk(0, True, False)
            with pool.Fori(1, NCH - 1) as c:
                chunk(c, False, False)
            chunk(NCH - 1, False, True)

        @block.sync
        def _(sp):
            def stage(p):
                before = p - SR
                if before in POOL_PIECES:
                    sp.wait_ge(k_low_pool, pool_pieces(before + 1))
                elif before >= 0:
                    sp.wait_ge(k_low, before + 1 - pool_pieces(before + 1))
                sp.dma_start(staging(p), kmat[:, p * KPIECE:(p + 1) * KPIECE]).then_inc(staged[p % SR], 16)

            def duplicate(c, m):
                prev, pm = (c, m - UR) if m >= UR else (c - 1, m - UR + NP)
                if positive(prev, NE, LAST_EVENT[pm] + 1):
                    sp.wait_ge(tile_done, count(prev, NE, LAST_EVENT[pm] + 1))
                    sp.sem_inc(ring_free, 1)
                sp.wait_ge(low_made, count(c, NP, m + 1))
                s = m % UR
                for f in range(2):
                    src = parts[f * D:(f + 1) * D, m % YR].bitcast(F32)
                    sp.dma_start(emb[0:D, s, f].bitcast(F32), src).then_inc(dup_in[s], 16)
                    sp.dma_start(emb[D:2 * D, s, f].bitcast(F32), src).then_inc(dup_in[s], 16)

            def spread_leaves(c, m):
                g = m // 2
                if positive(c - 1, NE, LAST_LEAF[g] + 1):
                    sp.wait_ge(mult_done, count(c - 1, NE, LAST_LEAF[g] + 1))
                    sp.sem_inc(leaves_free, 1)
                sp.wait_ge(prep_kept, count(c, NP, m + 1))
                strips = D * (m % 2)
                for half in range(2):
                    sp.dma_start(leaf_q[strips:strips + D, g, half * NB:(half + 1) * NB],
                                 plain[half::2, m % YR, :]).then_inc(leaf_in[m % YR], 16)

            def load_dense(c, z):
                sp.wait_ge(z_kept, count(c, NZ, z + 1))
                sp.sem_inc(block_free, 1)
                for g, slot in INNER_SLOT.items():
                    if slot // 16 == z:
                        row = z_place(slot, 0, 3)[1]
                        sp.dma_start(zs[row:row + 33:32, z, :], dense_v[c, 2 * g:2 * g + 2, :]).then_inc(dense_in, 16)

            def load_weights(c, step):
                if step >= WR:
                    sp.wait_ge(mlp_filled, count(c, NMLP, step - WR + 1))
                src = w1[step] if step < M1 else w2[step - M1]
                sp.dma_start(weights[:, step % WR], src).then_inc(weights_in[step % WR], 16)

            def store(c):
                sp.wait_ge(mlp_kept, count(c, NMLP, NMLP))
                sp.sem_inc(row_ready, 1)
                sp.dma_start(out_v[c], y_row).then_inc(out_stored, 16)

            def chunk(c, first, last):
                for e in range(NE):
                    if first:
                        for p in pieces_at(e):
                            if p + SR < NPIECE:
                                stage(p + SR)
                    for m in range(NP):
                        if DUP_AT.get(m) == e:
                            duplicate(c, m)
                        if DUP_NEXT.get(m) == e and not last:
                            duplicate(c + 1, m)
                        if LEAF_AT.get(m) == e:
                            spread_leaves(c, m)
                        if LEAF_NEXT.get(m) == e and not last:
                            spread_leaves(c + 1, m)
                    for z in range(NZ):
                        if e == 2 * Z_LAST[z] + LAG:
                            load_dense(c, z)
                        if e == 2 * Z_LAST[z] + LAG - NE and not first:
                            load_dense(c - 1, z)
                    if e == TAIL_WEIGHTS_AT and last:
                        sp.wait_ge(prep_filled, count(c, NP, NP))
                        for m in range(NP - YR, NP):
                            sp.wait_ge(dup_in[m % UR], count(c, 64 * NP // UR, 64 * (m // UR + 1)))
                        for step in range(M1 + M2):
                            src = w1[step] if step < M1 else w2[step - M1]
                            sp.dma_start(tail_weights(step), src).then_inc(tail_weights_in, 16)
                    for step, at in enumerate(WEIGHTS_AT):
                        if at == e and not first:
                            load_weights(c - 1, step)
                    if e == MLP_AT[-1] and not first:
                        store(c - 1)

            for p in range(SR):
                stage(p)
            sp.dma_start(ident[:], ident_in).then_inc(consts_in, 16)
            sp.dma_start(sel[:], sel_in).then_inc(consts_in, 16)
            sp.dma_start(b1_sb[:], b1).then_inc(consts_in, 16)
            sp.dma_start(b2_sb[:], b2).then_inc(consts_in, 16)
            sp.dma_start(w3_sb[:], w3).then_inc(consts_in, 16)
            for p in pieces_at(-1):
                if p + SR < NPIECE:
                    stage(p + SR)
            for m in range(4):
                if m in DUP_NEXT:
                    duplicate(0, m)
                spread_leaves(0, m)
            chunk(0, True, False)
            sp.wait_ge(k_low, NPIECE - len(POOL_PIECES))
            with sp.Fori(1, NCH - 1) as c:
                chunk(c, False, False)
            chunk(NCH - 1, False, True)
            load_dense(NCH - 1, NZ - 1)
            store(NCH - 1)
            sp.wait_ge(out_stored, 16 * NCH)

        @block.scalar
        def _(act):
            def k_high_part(p):
                act.wait_ge(staged[p % SR], 16 * (p // SR + 1))
                nc.scalar.copy(split_k[:, p * KPIECE:(p + 1) * KPIECE], staging(p)).then_inc(k_high, 1)

            def keep_prep(c, m):
                act.wait_ge(prep_filled, count(c, NP, m + 1))
                prev, pm = (c, m - YR) if m >= YR else (c - 1, m - YR + NP)
                if positive(prev, 64 * NP // UR, 64 * (pm // UR + 1)):
                    act.wait_ge(dup_in[pm % UR], count(prev, 64 * NP // UR, 64 * (pm // UR + 1)))
                if positive(prev, 32 * NP // YR, 32 * (pm // YR + 1)):
                    act.wait_ge(leaf_in[pm % YR], count(prev, 32 * NP // YR, 32 * (pm // YR + 1)))
                nc.scalar.copy(parts[:, m % YR, 0, :], misc[:, 0:NB]).then_inc(high_made, 1)
                nc.scalar.copy(plain[:, m % YR, :], misc[:, 0:NB]).then_inc(prep_kept, 1)

            def keep_z(c, z):
                act.wait_ge(selected, count(c, NBATCH, Z_LAST[z] + 1))
                if positive(c, NMLP, 0):
                    act.wait_ge(mlp_filled, count(c, NMLP, 0))
                nc.scalar.copy(zs[:, z, :], zacc[:, 0:NB]).then_inc(z_kept, 1)

            def keep_mlp(c, step, bank):
                act.wait_ge(mlp_filled, count(c, NMLP, step + 1))
                if step < M1:
                    if step == 0:
                        if positive(c, 16, 0):
                            act.wait_ge(out_stored, count(c, 16, 0))
                    nc.scalar.activation(h1[:, step, :], bank[:, 0:NB], ACT.Relu,
                                         bias=b1_sb[:, step:step + 1]).then_inc(mlp_kept, 1)
                elif step < M1 + M2:
                    k = step - M1
                    nc.scalar.activation(h2[:, k, :], bank[:, 0:NB], ACT.Relu,
                                         bias=b2_sb[:, k:k + 1]).then_inc(mlp_kept, 1)
                else:
                    nc.scalar.copy(y_row, bank[0:1, 0:NB]).then_inc(mlp_kept, 1)

            def chunk(c, first, last):
                for e in range(NE):
                    if first:
                        for p in pieces_at(e):
                            k_high_part(p)
                    for z in range(NZ):
                        if e == 2 * Z_LAST[z] + LAG:
                            keep_z(c, z)
                        if e == 2 * Z_LAST[z] + LAG - NE and not first:
                            keep_z(c - 1, z)
                    for m in range(NP):
                        if PREP_AT.get(m) == e:
                            keep_prep(c, m)
                        if PREP_NEXT.get(m) == e and not last:
                            keep_prep(c + 1, m)
                    if e in MLP_AT and not first:
                        keep_mlp(c - 1, MLP_AT.index(e), misc[:, :])

            for p in pieces_at(-1):
                k_high_part(p)
            for m in PREP_NEXT:
                keep_prep(0, m)
            act.wait_ge(consts_in, 16 * 5)
            chunk(0, True, False)
            with act.Fori(1, NCH - 1) as c:
                chunk(c, False, False)
            chunk(NCH - 1, False, True)
            keep_z(NCH - 1, NZ - 1)
            for step in range(NMLP):
                keep_mlp(NCH - 1, step, tail_bank(step))

        @block.vector
        def _(dve):
            def k_low_part(p):
                dve.wait_ge(k_high, p + 1)
                part = split_k[D:2 * D, p * KPIECE:(p + 1) * KPIECE]
                nc.vector.tensor_tensor(part, staging(p)[D:2 * D], part.bitcast(F32),
                                        ALU.subtract).then_inc(k_low, 1)

            def low_part(c, m):
                dve.wait_ge(high_made, count(c, NP, m + 1))
                dve.wait_ge(prep_kept, count(c, NP, m + 1))
                nc.vector.tensor_tensor(parts[:, m % YR, 1, :], plain[:, m % YR, :],
                                        parts[:, m % YR, 0, :].bitcast(F32), ALU.subtract).then_inc(low_made, 1)

            def multiply(c, e):
                ev = EVENTS[e]
                n = len(ev.owners)
                if e == FIRST_LEAF[ev.leaf]:
                    dve.wait_ge(leaf_in[0], count(c, 32 * NP // YR, 32 * (ev.leaf + 1)))
                    dve.wait_ge(leaf_in[1], count(c, 32 * NP // YR, 32 * (ev.leaf + 1)))
                if positive(c, NBATCH, (e - PR) // 2 + 1):
                    dve.wait_ge(selected, count(c, NBATCH, (e - PR) // 2 + 1))
                dve.wait_ge(tile_done, count(c, NE, e + 1))
                leaf = leaf_q[:, ev.leaf:ev.leaf + 1, :]
                nc.vector.tensor_tensor(
                    prod[:, e % PR, 0:n].rearrange("p o h b -> p o (h b)"),
                    tiles[e % XR][:, 0:n * FC].rearrange("p (o x) -> p o x", o=n),
                    leaf.to_broadcast([128, n, 2 * NB]) if n > 1 else leaf,
                    ALU.mult).then_inc(mult_done, 1)

            def fold(c, b):
                dve.wait_ge(mult_done, count(c, NE, 2 * b + 2))
                s = 2 * b % PR
                nc.vector.tensor_tensor(prod[:, s:s + 2, :, 0], prod[:, s:s + 2, :, 0], prod[:, s:s + 2, :, 1],
                                        ALU.add).then_inc(folded, 1)

            def chunk(c, first, last):
                for e in range(NE):
                    multiply(c, e)
                    if e // 2 in FOLDED and e % 2 and not first:
                        fold(c, e // 2)
                    for m in range(NP):
                        if PREP_AT.get(m) == e:
                            low_part(c, m)
                        if PREP_NEXT.get(m) == e and not last:
                            low_part(c + 1, m)
                    if first:
                        for p in pieces_at(e):
                            if p not in POOL_PIECES:
                                k_low_part(p)

            for p in pieces_at(-1):
                k_low_part(p)
            for m in PREP_NEXT:
                low_part(0, m)
            chunk(0, True, False)
            with dve.Fori(1, NCH - 1) as c:
                chunk(c, False, False)
            chunk(NCH - 1, False, True)

        @block.tensor
        def _(pe):
            def bilinear(c, e, first):
                ev = EVENTS[e]
                if e == FIRST_EVENT[ev.pair]:
                    pe.wait_ge(dup_in[ev.pair % UR], count(c, 64 * NP // UR, 64 * (ev.pair // UR + 1)))
                if first:
                    n = pool_pieces(pieces_needed(e))
                    pe.wait_ge(k_low, pieces_needed(e) - n)
                    if n:
                        pe.wait_ge(k_low_pool, n)
                if positive(c, NE, e - XR + 1):
                    pe.wait_ge(mult_done, count(c, NE, e - XR + 1))
                for o, f, _ in ev.owners:
                    col, n = KAT[2 * ev.pair + f, ev.leaf]
                    for half in range(2):
                        at = col + half * n * H
                        dst = tiles[e % XR][:, o * FC + half * NB:o * FC + (half + 1) * NB]
                        nc.tensor.matmul(dst, split_k[:, at:at + 128], emb[:, ev.pair % UR, f, 0, :],
                                         start=True, stop=False)
                        last = nc.tensor.matmul(dst, split_k[:, at:at + 128], emb[:, ev.pair % UR, f, 1, :],
                                                start=False, stop=True)
                last.then_inc(tile_done, 1)

            def select(c, b, folds=True):
                pair = [2 * b, 2 * b + 1]
                z = EVENTS[pair[0]].slot // 16
                if b == (Z_LAST[z - 1] + 1 if z else 0):
                    if positive(c, NZ, z):
                        pe.wait_ge(z_kept, count(c, NZ, z))
                halves = 2
                if b in FOLDED and folds:
                    halves = 1
                    pe.wait_ge(folded, count(c - 1, NFOLD, FOLDED.index(b) + 1))
                todo = []
                for half in range(halves):
                    for e in pair:
                        ev = EVENTS[e]
                        for o, _, live in ev.owners:
                            todo.append((half, e, o, live))
                for half, e, o, live in todo:
                    ev = EVENTS[e]
                    strip = z_place(ev.slot, o, 0)[1] // 32
                    row = 4 * (ev.slot // 2 % 8) + (2 if ev.kind == "single" else 0)
                    use = [(n, h, oo) for n, x in enumerate(EVENTS) for h in range(1 if n // 2 in FOLDED and folds else 2) for oo, _, _ in x.owners
                           if x.slot // 16 == z and z_place(x.slot, oo, 0)[1] // 32 == strip]
                    key = lambda t: (t[0] // 2, t[1], t[0], t[2])
                    first, final = min(use, key=key), max(use, key=key)
                    last = nc.tensor.matmul(
                        zacc[32 * strip:32 * strip + 32, 0:NB],
                        sel[:, LEAVES.index(live), 32 - row:64 - row], prod[:, e % PR, o, half, :],
                        start=(e, half, o) == first, stop=(e, half, o) == final)
                last.then_inc(selected, 1)

            def prepare(c, m):
                if positive(c, NP, m):
                    pe.wait_ge(prep_kept, count(c, NP, m))
                g, f = m // 2, GF // 2 * (m % 2)
                pe.wait_ge(gathered[g % ER], count(c, 2 * GF * BT * 16, (g // ER + 1) * GF * BT * 16))
                for t in range(BT):
                    last = nc.tensor.transpose(misc[:, t * 128:(t + 1) * 128],
                                               rows[:, g % ER, t, f:f + 2, :].rearrange("p f d -> p (f d)"), ident[:])
                last.then_inc(prep_filled, 1)

            def perceptron(c, step):
                if positive(c, NMLP, step):
                    pe.wait_ge(mlp_kept, count(c, NMLP, step))
                if step < M1 + M2:
                    uses = (M1 + M2) // WR
                    pe.wait_ge(weights_in[step % WR], count(c, 16 * uses, 16 * (step // WR + 1)))
                if step < M1:
                    if step == 0:
                        pe.wait_ge(z_kept, count(c, NZ, NZ))
                        pe.wait_ge(dense_in, count(c, 16 * NG, 16 * NG))
                    for z in range(NZ):
                        last = nc.tensor.matmul(misc[:, 0:NB], weights[:, step % WR, z, :],
                                                zs[:, z, :], start=(z == 0), stop=(z == NZ - 1))
                elif step < M1 + M2:
                    for k in range(M1):
                        last = nc.tensor.matmul(misc[:, 0:NB], weights[:, step % WR, k, :],
                                                h1[:, k, :], start=(k == 0), stop=(k == M1 - 1))
                else:
                    for k in range(M2):
                        last = nc.tensor.matmul(misc[0:1, 0:NB], w3_sb[:, k:k + 1], h2[:, k, :],
                                                start=(k == 0), stop=(k == M2 - 1))
                last.then_inc(mlp_filled, 1)

            def chunk(c, first, last):
                for e in range(NE):
                    bilinear(c, e, first)
                    if e % 2 and e >= LAG:
                        select(c, (e - LAG) // 2, not first)
                    elif e % 2 and not first:
                        select(c - 1, (e - LAG) // 2 + NBATCH)
                    for m in range(NP):
                        if PREP_AT.get(m) == e:
                            if not first:
                                before = sum(x < e for x in MLP_AT)
                                if positive(c - 1, NMLP, before):
                                    pe.wait_ge(mlp_kept, count(c - 1, NMLP, before))
                            prepare(c, m)
                        if PREP_NEXT.get(m) == e and not last:
                            prepare(c + 1, m)
                    if e in MLP_AT and not first:
                        before = len(PREP_NEXT) + sum(x <= e for x in PREP_AT.values())
                        if positive(c, NP, before):
                            pe.wait_ge(prep_kept, count(c, NP, before))
                        perceptron(c - 1, MLP_AT.index(e))

            pe.wait_ge(consts_in, 16 * 5)
            for m in PREP_NEXT:
                prepare(0, m)
            chunk(0, True, False)
            with pe.Fori(1, NCH - 1) as c:
                chunk(c, False, False)
            chunk(NCH - 1, False, True)
            c, z = NCH - 1, NZ - 1

            def first_layer(step, blocks):
                for k in blocks:
                    last = nc.tensor.matmul(tail_bank(step)[:, 0:NB], tail_weights(step)[:, k, :], zs[:, k, :],
                                            start=(k == 0), stop=(k == z))
                return last

            for b in range(NBATCH - LAG // 2, NBATCH - 1):
                pe.wait_ge(mult_done, count(c, NE, 2 * b + 2))
                select(c, b)
            pe.wait_ge(tail_weights_in, 16 * (M1 + M2))
            pe.wait_ge(z_kept, count(c, NZ, z))
            pe.wait_ge(dense_in, count(c, 16 * NG, 16 * sum(slot // 16 < z for slot in INNER_SLOT.values())))
            pe.wait_ge(mult_done, count(c, NE, NE - 2))
            first_layer(0, range(z))
            first_layer(1, range(z))
            pe.wait_ge(mult_done, count(c, NE, NE))
            select(c, NBATCH - 1)
            first_layer(2, range(z))
            first_layer(3, range(z))
            pe.wait_ge(z_kept, count(c, NZ, NZ))
            pe.wait_ge(dense_in, count(c, 16 * NG, 16 * NG))
            for step in range(M1):
                first_layer(step, [z]).then_inc(mlp_filled, 1)
            for step in range(M1, M1 + M2):
                for k in range(M1):
                    pe.wait_ge(mlp_kept, count(c, NMLP, k + 1))
                    last = nc.tensor.matmul(tail_bank(step)[:, 0:NB], tail_weights(step)[:, k, :], h1[:, k, :],
                                            start=(k == 0), stop=(k == M1 - 1))
                last.then_inc(mlp_filled, 1)
            for k in range(M2):
                pe.wait_ge(mlp_kept, count(c, NMLP, M1 + k + 1))
                last = nc.tensor.matmul(tail_bank(NMLP - 1)[0:1, 0:NB], w3_sb[:, k:k + 1], h2[:, k, :],
                                        start=(k == 0), stop=(k == M2 - 1))
            last.then_inc(mlp_filled, 1)


def layouts():
    def pair_number(j, i):
        return j * (2 * F - j - 1) // 2 + i - j - 1

    col_n, col_e = np.zeros(KCOLS, np.int64), np.zeros(KCOLS, np.int64)
    for (i, g), (col, n) in KAT.items():
        for half in range(2):
            for k in range(n):
                at = col + (half * n + k) * H
                col_n[at:at + H] = pair_number(GF * g + k, i)
                col_e[at:at + H] = 2 * np.arange(H) + half
    w1_row = np.full((128, NZ), -1, np.int64)
    for ev in EVENTS:
        for o, f, live in ev.owners:
            for k in range(live):
                z, row = z_place(ev.slot, o, k + (2 if ev.kind == "single" else 0))
                w1_row[row, z] = pair_number(GF * ev.leaf + k, 2 * ev.pair + f)
    for g, slot in INNER_SLOT.items():
        for o in range(2):
            z, row = z_place(slot, o, 3)
            w1_row[row, z] = F * (F - 1) // 2 + 2 * g + o
    assert sorted(w1_row.ravel()) == list(range(N1))
    sel = np.zeros((128, len(LEAVES), SELW), np.float32)
    for n, live in enumerate(LEAVES):
        for p in range(live * H):
            sel[p, n, 32 + p // H] = 1.0
    return col_n, col_e, w1_row, sel


def kernel(**inputs):
    import concourse.bacc as _bacc
    from concourse.bass_utils import run_bass_kernel_spmd as _run

    col_n, col_e, w1_row, sel = layouts()
    get = lambda name: np.asarray(inputs[name])
    arrays = {
        "dense_t": np.ascontiguousarray(get("dense_ctx").T),
        "ids": np.ascontiguousarray(get("ids")),
        "w1": np.ascontiguousarray(get("W_top1")[w1_row].reshape(128, NZ, M1, 128).transpose(2, 0, 1, 3)),
        "b1": np.ascontiguousarray(get("b_top1").reshape(M1, 128).T),
        "w2": np.ascontiguousarray(get("W_top2").reshape(M1, 128, M2, 128).transpose(2, 1, 0, 3)),
        "b2": np.ascontiguousarray(get("b_top2").reshape(M2, 128).T),
        "w3": np.ascontiguousarray(get("W_top3").reshape(M2, 128).T),
        "kmat": np.tile(get("L0_rec_kernel")[:, col_n, col_e], (2, 1)),
        "ident": np.eye(128, dtype=np.float32),
        "sel": sel,
    }
    for f in range(F):
        arrays[f"tbl_{f}"] = np.ascontiguousarray(get(f"tbl_{f}"))
    nc = _bacc.Bacc("TRN2", target_bir_lowering=False, num_devices=1)
    aps = {}
    for name, a in arrays.items():
        dt = U32 if name == "ids" else mybir.dt.from_np(a.dtype)
        aps[name] = nc.dram_tensor("in_" + name, a.shape, dt, kind="ExternalInput").ap()
    arrays["ids"] = arrays["ids"].view(np.uint32)
    out = nc.dram_tensor("out", (B, 1), F32, kind="ExternalOutput").ap()
    dlrm_tower(nc, aps["dense_t"], aps["ids"], [aps[f"tbl_{f}"] for f in range(F)], aps["w1"], aps["b1"],
               aps["w2"], aps["b2"], aps["w3"], aps["kmat"], aps["ident"], aps["sel"], out)
    r = _run(nc, [{"in_" + name: a for name, a in arrays.items()}], core_ids=[0])
    return r.results[0]["out"]
```
